# Optimizing a Trainium2 kernel written in Bass

```python
import numpy as np
import jax
import jax.numpy as jnp

def _softmax(x, axis=-1):
    return jax.nn.softmax(x, axis=axis)

def _gelu(x):
    return jax.nn.gelu(x, approximate=True)

def _silu(x):
    return jax.nn.silu(x)

def _sigmoid(x):
    return jax.nn.sigmoid(x)

def _layernorm(x, axis=-1, eps=1e-05):
    m = jnp.mean(x, axis=axis, keepdims=True)
    v = jnp.var(x, axis=axis, keepdims=True)
    return (x - m) / jnp.sqrt(v + eps)

def _scatter_add(tgt, idx, src, axis=0):
    return tgt.at[idx].add(src)

def _segment_sum(src, seg, n):
    return jax.ops.segment_sum(src, seg, n)
kernel_name = 'mk_gnn_ffn_d1_gnn_r8_f5a00d'

def setup_inputs(seed: int=0):
    np.random.seed(seed)
    _w = jnp.asarray

    def _rec_inputs():
        import jax
        import jax.numpy as jnp
        _gk = jax.random.key(seed)
        x = -0.000202 + 1 * jax.random.normal(jax.random.fold_in(_gk, 1), (6250, 256), jnp.float32)
        src = jax.random.randint(jax.random.fold_in(_gk, 2), (200000,), 0, 6250, jnp.int32)
        dst = jax.random.randint(jax.random.fold_in(_gk, 3), (200000,), 0, 6250, jnp.int32)
        _o = jnp.argsort(dst, stable=True)
        src = src[_o]
        dst = dst[_o]
        return (x, src, dst)
    x, src, dst = _rec_inputs()

    def _L0_gnn_setup():
        import jax, jax.numpy as jnp
        import numpy as np
        N_NODES = 3125
        N_EDGES = 50000
        D = 256
        key = jax.random.key(seed)
        k1, k2, k3, k4, k5 = jax.random.split(key, 5)
        feat = jax.random.normal(k1, (N_NODES, D), dtype=jnp.float32)
        src = jax.random.randint(k2, (N_EDGES,), 0, N_NODES, dtype=jnp.int32)
        dst = jax.random.randint(k3, (N_EDGES,), 0, N_NODES, dtype=jnp.int32)
        a = float(np.sqrt(6.0 / (D + D)))
        W1 = jax.random.uniform(k4, (D, D), minval=-a, maxval=a, dtype=jnp.float32)
        W2 = jax.random.uniform(k5, (D, D), minval=-a, maxval=a, dtype=jnp.float32)
        b = jnp.zeros((D,), dtype=jnp.float32)
        return {'feat': feat, 'W1': W1, 'W2': W2, 'b': b, 'src': src, 'dst': dst}
    _L0_gnn_all = _L0_gnn_setup()
    _L0_gnn_in = {k: v for k, v in _L0_gnn_all.items() if k in ('W1', 'W2', 'b')}
    del _L0_gnn_all

    def _L0_ffn_setup():
        import jax, jax.numpy as jnp
        import numpy as np
        B, S, D, E, H, K = (4, 512, 256, 8, 512, 2)
        key = jax.random.key(seed)
        ks = jax.random.split(key, 6)
        x = jax.random.normal(ks[0], (B, S, D), jnp.float32)
        Wg = jax.random.normal(ks[1], (D, E), jnp.float32) * 0.02
        bg = jnp.zeros((E,), jnp.float32)
        W1 = jax.random.normal(ks[2], (E, D, H), jnp.float32) * 0.02
        b1 = jnp.zeros((E, H), jnp.float32)
        W2 = jax.random.normal(ks[3], (E, H, D), jnp.float32) * 0.02
        b2 = jnp.zeros((E, D), jnp.float32)
        return {'x': x, 'Wg': Wg, 'bg': bg, 'W1': W1, 'b1': b1, 'W2': W2, 'b2': b2}
    _L0_ffn_all = _L0_ffn_setup()
    _L0_ffn_in = {k: v for k, v in _L0_ffn_all.items() if k in ('Wg', 'bg', 'W1', 'b1', 'W2', 'b2')}
    del _L0_ffn_all
    return {'x': x, 'src': src, 'dst': dst, 'L0_gnn_W1': _L0_gnn_in['W1'], 'L0_gnn_W2': _L0_gnn_in['W2'], 'L0_gnn_b': _L0_gnn_in['b'], 'L0_ffn_Wg': _L0_ffn_in['Wg'], 'L0_ffn_bg': _L0_ffn_in['bg'], 'L0_ffn_W1': _L0_ffn_in['W1'], 'L0_ffn_b1': _L0_ffn_in['b1'], 'L0_ffn_W2': _L0_ffn_in['W2'], 'L0_ffn_b2': _L0_ffn_in['b2']}

def reference(x, src, dst, L0_gnn_W1, L0_gnn_W2, L0_gnn_b, L0_ffn_Wg, L0_ffn_bg, L0_ffn_W1, L0_ffn_b1, L0_ffn_W2, L0_ffn_b2):
    import jax
    import jax.numpy as jnp

    def _L0_gnn_ref(feat, W1, W2, b, src, dst):
        import jax, jax.numpy as jnp
        import numpy as np
        N_NODES = 3125
        N_EDGES = 50000
        D = 256
        n = feat.shape[0]
        ones = jnp.ones(src.shape[0], dtype=feat.dtype)
        out_deg = jnp.maximum(jax.ops.segment_sum(ones, src, num_segments=n), 1.0)
        in_cnt = jax.ops.segment_sum(ones, dst, num_segments=n)
        t1 = feat @ W1
        msg = t1[src] + feat[src] * feat[dst] @ W2
        scale = jnp.sqrt(out_deg[src]) * jnp.sqrt(out_deg[dst])
        msg = msg / scale[:, None]
        agg = jax.ops.segment_sum(msg, dst, num_segments=n)
        embed = jnp.where(in_cnt[:, None] > 0, t1 + agg, jnp.zeros_like(t1))
        embed = embed + b
        embed = jax.nn.leaky_relu(embed, negative_slope=0.01)
        norm = jnp.linalg.norm(embed, axis=1, keepdims=True)
        embed = embed / jnp.maximum(norm, 1e-12)
        return embed

    def _L0_ffn_ref(x, Wg, bg, W1, b1, W2, b2):
        import jax, jax.numpy as jnp
        import numpy as np
        B, S, D, E, H, K = (4, 512, 256, 8, 512, 2)
        Bv, Sv, Dv = x.shape
        gate_scores = x @ Wg + bg
        _, idx = jax.lax.top_k(gate_scores, K)
        mask = jax.nn.one_hot(idx, E, dtype=x.dtype).sum(axis=-2)
        xf = x.reshape(-1, Dv)
        mf = mask.reshape(-1, E)
        h = jax.nn.gelu(jnp.einsum('td,edh->teh', xf, W1) + b1[None], approximate=False)
        y = jnp.einsum('teh,ehd->ted', h, W2) + b2[None]
        out = jnp.einsum('ted,te->td', y, mf)
        return out.reshape(Bv, Sv, Dv)
    x = x + _L0_gnn_ref(_layernorm(x, axis=-1), L0_gnn_W1, L0_gnn_W2, L0_gnn_b, src, dst)
    x = x + _L0_ffn_ref(_layernorm(x, axis=-1)[None], L0_ffn_Wg, L0_ffn_bg, L0_ffn_W1, L0_ffn_b1, L0_ffn_W2, L0_ffn_b2)[0]
    return x

_drawn_inputs = setup_inputs


def setup_inputs(seed=0):
    import zlib

    import numpy as np

    out = dict(_drawn_inputs(seed))
    spreads = {'L0_gnn_b': (0.0, 0.439),
     'L0_ffn_bg': (0.0, 0.1),
     'L0_ffn_b1': (0.0, 0.1),
     'L0_ffn_b2': (0.0, 0.1)}
    factors = {'L0_gnn_W2': 2.767}
    for name, (base, spread) in spreads.items():
        noise = np.random.default_rng([zlib.crc32(name.encode()), seed]).standard_normal(out[name].shape)
        drawn = base * np.exp(spread * noise) if base else spread * noise
        out[name] = jnp.asarray(drawn.astype(out[name].dtype))
    for name, factor in factors.items():
        out[name] = (out[name] * factor).astype(out[name].dtype)
    return out
```

```python
from contextlib import ExitStack

import concourse.bass as bass
from concourse import mybir

F32 = mybir.dt.float32
BF16 = mybir.dt.bfloat16
F16 = mybir.dt.float16
I32 = mybir.dt.int32
U32 = mybir.dt.uint32
ALU = mybir.AluOpType
ACT = mybir.ActivationFunctionType
AX = mybir.AxisListType

P = 128
EPS = 1e-5
TPG = 7
GE = TPG * P
GPI = 9
RING = 3
WIN = 64
NB = 250
SUB = 125
LEAD = 2
HC_COLS = 32
YSCALE = 64.0


def steps(eng, sem, base):
    at = [0]

    def link(ins, after=None):
        at[0] += 1
        ins.then_inc(sem, 1)
        eng.wait_ge(sem, base + at[0])
        if after:
            after(eng)
    link.at = at
    return link


def bass_gnn_ffn(nc, x, src, dst, gw1, gw2, gb, wg, bg, w1, b1, w2, b2, out):
    N, D = x.shape
    NE = src.shape[0]
    E, _, H = w1.shape
    KC = D // P
    HCH = H // P
    NBLK = N // NB
    FULL = NE // GE
    NG = FULL + 1
    SHORT_TILES = 2
    SHORT = (NE - FULL * GE) // SHORT_TILES
    LASTJ = (NG - 1) // GPI
    LASTK = (NG - 1) % GPI
    ACCW = N + WIN
    RT = N // SUB
    XC = 5
    TC = RT // XC
    YC = 10
    TY = RT // YC
    YBUF = 4
    HCOL = NE // SUB
    LO = 64
    HI = -(-N // LO)
    MG = NG // 2
    assert NBLK * NB == N and NG % 2 == 0 and KC == 2 and SHORT * SHORT_TILES + FULL * GE == NE and SHORT <= P
    assert LASTJ == NBLK - 1 and HCOL % (2 * HC_COLS) == 0 and RT * SUB == N

    y_tab = nc.dram_tensor("y_tab", (N, 2 * D), F16, kind="Internal").ap()
    xn_tab = nc.dram_tensor("xn_tab", (N, D), F32, kind="Internal").ap()
    deg_tab = nc.dram_tensor("deg_tab", (HI * LO,), F32, kind="Internal").ap()
    r_tab = nc.dram_tensor("r_tab", (N,), F32, kind="Internal").ap()
    min_tab = nc.dram_tensor("min_tab", (NG,), I32, kind="Internal").ap()
    max_tab = nc.dram_tensor("max_tab", (NG,), I32, kind="Internal").ap()

    with ExitStack() as ctx:
        def sb(name, shape, dt=F32):
            return ctx.enter_context(nc.sbuf_tensor(name, shape, dt))

        def psum(name, shape):
            return ctx.enter_context(nc.psum_tensor(name, shape, F32))

        def sem(name):
            return ctx.enter_context(nc.semaphore(name))

        acc = sb("acc", [P, 3 * ACCW])
        acc3 = acc[:, :].rearrange("p (c n) -> p c n", c=3)
        wts = sb("wts", [P, E * (KC * H + HCH * D)])
        w1_sb = wts[:, 0:E * KC * H].rearrange("p (e k h) -> p e k h", e=E, k=KC)
        w2_sb = wts[:, E * KC * H:].rearrange("p (e c d) -> p e c d", e=E, c=HCH)
        ring = sb("ring", [P, RING, TPG, D])
        ring16 = ring[:, :, :, :].bitcast(F16)
        idx = sb("idx", [P, GPI, TPG], U32)
        dst_i = sb("dst_i", [P, GPI, TPG], I32)
        idx_s = sb("idx_s", [SHORT, SHORT_TILES], U32)
        dst_s = sb("dst_s", [SHORT, SHORT_TILES], I32)
        loc = sb("loc", [P, RING, TPG])
        oh = sb("oh", [P, RING, TPG, WIN], F16)
        gw_sb = sb("gw_sb", [P, 2, KC, D])
        gb_b = sb("gb_b", [SUB, D])
        wg_sb = sb("wg_sb", [P, KC, E])
        bg_b = sb("bg_b", [SUB, E])
        b1_sb = sb("b1_sb", [P, E, HCH])
        b2_sb = sb("b2_sb", [E, D])
        x_blk = sb("x_blk", [SUB, 2, D])
        xn_blk = sb("xn_blk", [SUB, 2, D])
        r_blk = sb("r_blk", [P, NB])
        rs = sb("rs", [P, KC, NB])
        u_t = sb("u_t", [P, KC, NB])
        v_t = sb("v_t", [P, KC, NB])
        emb = sb("emb", [SUB, 2, D])
        junk = sb("junk", [SUB, 2, D], BF16)
        x1 = sb("x1", [SUB, 2, D])
        xn2T = sb("xn2T", [P, KC, NB])
        gelu = sb("gelu", [P, 2, HCH, NB])
        accy = sb("accy", [SUB, 2, D])
        outb = sb("outb", [SUB, 2, D])
        ssq = sb("ssq", [SUB, 2])
        rn = sb("rn", [SUB, 2])
        stats = sb("stats", [SUB, 2, 6])
        mv = sb("mv", [SUB, 2, 2])
        rstd2 = sb("rstd2", [SUB, 2])
        score = sb("score", [SUB, 2, E])
        top = sb("top", [SUB, 2, 8])
        topi = sb("topi", [SUB, 2, 8], U32)
        topf = sb("topf", [SUB, 2, 8])
        mask = sb("mask", [SUB, 2, E])
        maskT = sb("maskT", [E, 2, SUB])
        ident = sb("ident", [P, P])
        iota_w = sb("iota_w", [P, WIN])
        iota_8 = sb("iota_8", [SUB, E])
        iota_nb = sb("iota_nb", [P, NB])
        blk0 = sb("blk0", [P, NBLK])
        ones = sb("ones", [P, P], F16)
        zeros = sb("zeros", [P, P], BF16)
        base_i = sb("base_i", [1, NG], I32)
        base_f = sb("base_f", [P, NG])
        flag_f = sb("flag_f", [1, 2])
        flag = sb("flag", [1, 1], I32)
        xbuf = wts[0:SUB, 0:RT * D].rearrange("p (t d) -> p t d", d=D)
        hi_b = wts[0:SUB, RT * D:RT * D + HCOL // 2].bitcast(BF16)
        lo_b = wts[0:SUB, RT * D + HCOL // 2:RT * D + HCOL].bitcast(BF16)
        YW = TY * D
        ybuf = [wts[0:SUB, RT * D + n * YW:RT * D + (n + 1) * YW].bitcast(F16).rearrange("p (t c) -> p t c", c=2 * D)
                for n in range(2)]
        ybuf += [ring16[0:SUB, 1 + n:2 + n, 0:TY, :].rearrange("p a t c -> p (a t) c") for n in range(2)]
        r_small = sb("r_small", [SUB, RT])
        rows0 = ring[:, 0:1, :, :].rearrange("p a t d -> p (a t) d")
        base_bi = rows0[:, 0, 0:NG].bitcast(I32)
        max_i = rows0[0:1, 1, 0:NG].bitcast(I32)
        thr = rows0[0:1, 2, :]
        span = rows0[0:1, 3, 0:NG]
        late = rows0[0:1, 4, 0:NG]
        a0 = 0

        def part(n):
            nonlocal a0
            a0 += n
            return acc[:, a0 - n:a0]
        src_i = part(HCOL)[0:SUB].bitcast(U32)
        hi_i = part(HCOL)[0:SUB].bitcast(U32)
        lo_i = part(HCOL)[0:SUB].bitcast(U32)
        iota_v = part(HI * HC_COLS // 2)[0:SUB].bitcast(BF16).rearrange("p (v c) -> p v c", c=HC_COLS)
        oh_hi = part(HI * HC_COLS)[0:SUB].bitcast(BF16).rearrange("p (b v c) -> p b v c", b=2, c=HC_COLS)
        oh_lo = part(LO * HC_COLS)[0:SUB].bitcast(BF16).rearrange("p (b v c) -> p b v c", b=2, c=HC_COLS)
        junk_t = part(TC * D // 2)[0:SUB].bitcast(BF16).rearrange("p (t d) -> p t d", d=D)
        dst_g = part(2 * GE)[0:MG].bitcast(I32).rearrange("p (s e) -> p s e", s=2)
        gmin = sb("gmin", [MG, 2], I32)
        gmax = sb("gmax", [MG, 2], I32)
        deg_hl = sb("deg_hl", [HI, LO])
        deg = rows0[0:SUB, 5, 0 * RT:1 * RT]
        r_col = rows0[0:SUB, 5, 1 * RT:2 * RT]
        negmean = rows0[0:SUB, 5, 2 * RT:3 * RT]
        rowsum = rows0[0:SUB, 5, 3 * RT:4 * RT]
        rowsq = rows0[0:SUB, 5, 4 * RT:5 * RT]
        std = rows0[0:SUB, 6, 0 * RT:1 * RT]
        rstd = rows0[0:SUB, 6, 1 * RT:2 * RT]
        nmr = rows0[0:SUB, 6, 2 * RT:3 * RT]
        eps_t = sb("eps_t", [SUB, 1])

        ps_g = psum("ps_g", [P, RING, 512])
        ps_h = psum("ps_h", [P, 2, 512])
        ps_y = psum("ps_y", [P, 2, 512])
        ps_a = psum("ps_a", [P, 512])
        hist = ps_a[0:HI, 0:LO]
        xnT_ps = ps_a[:, 0:KC * NB].rearrange("p (k n) -> p k n", k=KC)
        z_ps = ps_a[0:SUB, :].rearrange("p (s d) -> p s d", s=2)
        gate_ps = ps_a[0:SUB, 0:2 * E].rearrange("p (s e) -> p s e", s=2)
        maskT_ps = ps_a[0:E, 0:NB].rearrange("p (s n) -> p s n", s=2)

        src_in = sem("src_in")
        x_in = [sem(f"x_in{c}") for c in range(XC)]
        dst_in = sem("dst_in")
        const_in = sem("const_in")
        pool_const = sem("pool_const")
        hist_prep = sem("hist_prep")
        hist_oh = sem("hist_oh")
        hist_used = sem("hist_used")
        hist_done = sem("hist_done")
        minmax_done = sem("minmax_done")
        minmax_out = sem("minmax_out")
        base_in = sem("base_in")
        flag_chain = sem("flag_chain")
        flag_ready = sem("flag_ready")
        deg_done = sem("deg_done")
        deg_out = sem("deg_out")
        deg_in = sem("deg_in")
        deg_root = sem("deg_root")
        r_ready = sem("r_ready")
        r_out = sem("r_out")
        ln_sum = sem("ln_sum")
        ln_neg = sem("ln_neg")
        ln_sq = sem("ln_sq")
        ln_std = sem("ln_std")
        ln_scale = sem("ln_scale")
        xn_ready = sem("xn_ready")
        xn_out = [sem(f"xn_out{c}") for c in range(XC)]
        y_scaled = sem("y_scaled")
        y_high = sem("y_high")
        y_out = [sem(f"y_out{n}") for n in range(YBUF)]
        acc_zero = sem("acc_zero")
        w_in = sem("w_in")
        idx_in = [sem(f"idx_in{c}") for c in range(3)]
        gathered = [sem(f"gathered{s}") for s in range(RING)]
        loc_ready = sem("loc_ready")
        onehot = sem("onehot")
        summed = sem("summed")
        added = sem("added")
        blk_in = sem("blk_in")
        xnT_ready = sem("xnT_ready")
        uv_chain = sem("uv_chain")
        uv_ready = sem("uv_ready")
        z_ready = sem("z_ready")
        z_chain = sem("z_chain")
        emb_ready = sem("emb_ready")
        ssq_ready = sem("ssq_ready")
        ssq_floor = sem("ssq_floor")
        norm_ready = sem("norm_ready")
        var_ready = sem("var_ready")
        std2_ready = sem("std2_ready")
        x1_done = sem("x1_done")
        xn2_ready = sem("xn2_ready")
        xn2T_done = sem("xn2T_done")
        xn2T_ready = sem("xn2T_ready")
        gate_done = sem("gate_done")
        gate_chain = sem("gate_chain")
        mask_ready = sem("mask_ready")
        maskT_done = sem("maskT_done")
        maskT_ready = sem("maskT_ready")
        b2_done = sem("b2_done")
        init_done = sem("init_done")
        hid_ready = sem("hid_ready")
        gelu_done = sem("gelu_done")
        y_ready = sem("y_ready")
        y_added = sem("y_added")
        stored = sem("stored")
        waited = sem("waited")
        gen_idx = sem("gen_idx")
        gen_rows = sem("gen_rows")
        gen_loc = sem("gen_loc")
        gen_oh = sem("gen_oh")
        gen_sum = sem("gen_sum")
        gen_acc = sem("gen_acc")
        gen_hot = ring16[:, 1:2, :, :].rearrange("p a t d -> p (a t) d")[:, :, 0:NB]

        def settle(eng):
            eng.sem_inc(waited, 1)

        def path_flag(eng):
            eng.wait_ge(flag_ready, 1)
            return eng.value_load(flag[0:1, 0:1], min_val=0, max_val=1)

        def y_written(eng):
            for n in range(YBUF):
                eng.wait_ge(y_out[n], 16 * len(range(n, YC, YBUF)))

        block = ctx.enter_context(nc.Block())

        x_rows = x.rearrange("(p t) d -> p t d", t=RT)
        y_rows = y_tab.rearrange("(p t) c -> p t c", t=RT)
        xn_rows = xn_tab.rearrange("(p t) d -> p t d", t=RT)
        src_g = src[0:FULL * GE].rearrange("(g p j) -> p g j", p=P, j=TPG)
        dst_gr = dst[0:FULL * GE].rearrange("(g p j) -> p g j", p=P, j=TPG)
        src_sh = src[FULL * GE:NE].rearrange("(p j) -> p j", j=SHORT_TILES)
        dst_sh = dst[FULL * GE:NE].rearrange("(p j) -> p j", j=SHORT_TILES)
        ADD_INIT = 1

        def known(v, low):
            return not isinstance(v, int) or v >= low

        def shape_of(k, last):
            return (SHORT_TILES, SHORT) if last and k == LASTK else (TPG, P)

        @block.sync
        def _(sp):
            sp.dma_start(src_i, src.rearrange("(p c) -> p c", c=HCOL)).then_inc(src_in, 16)
            for c in range(XC):
                sp.dma_start(xbuf[:, c * TC:(c + 1) * TC, :], x_rows[:, c * TC:(c + 1) * TC, :]).then_inc(x_in[c], 16)
            whole = (MG - 1) * 2 * GE
            rest = NE - whole
            dg = dst_g.rearrange("p s e -> p (s e)")
            sp.dma_start(dg[0:MG - 1, :], dst[0:whole].rearrange("(p c) -> p c", c=2 * GE)).then_inc(dst_in, 16)
            sp.dma_start(dg[MG - 1:MG, 0:rest], dst[whole:NE].rearrange("(a c) -> a c", a=1)).then_inc(dst_in, 16)
            sp.dma_start(dg[MG - 1:MG, rest:2 * GE], dst[NE - (2 * GE - rest):NE].rearrange("(a c) -> a c", a=1)).then_inc(dst_in, 16)
            sp.dma_start(gw_sb[:, 0, :, :], gw1.rearrange("(k p) d -> p k d", p=P)).then_inc(const_in, 16)
            sp.dma_start(gw_sb[:, 1, :, :], gw2.rearrange("(k p) d -> p k d", p=P)).then_inc(const_in, 16)
            sp.dma_start(gb_b[:, :], gb.rearrange("(a d) -> a d", a=1).broadcast_to([SUB, D])).then_inc(const_in, 16)
            sp.dma_start(wg_sb[:, :, :], wg.rearrange("(k p) e -> p k e", p=P)).then_inc(const_in, 16)
            sp.dma_start(bg_b[:, :], bg.rearrange("(a d) -> a d", a=1).broadcast_to([SUB, E])).then_inc(const_in, 16)
            sp.dma_start(b1_sb[:, :, :], b1[:, :, :]).then_inc(const_in, 16)
            sp.dma_start(b2_sb[:, :], b2[:, :]).then_inc(const_in, 16)
            def load_chunk(j, c):
                g = 3 * c
                k0 = j * GPI + g
                if isinstance(j, int) and j == LASTJ and g + 2 >= LASTK:
                    n = LASTK - g
                    pairs = [(idx[:, g:g + n, :], src_g[:, k0:k0 + n, :]), (dst_i[:, g:g + n, :], dst_gr[:, k0:k0 + n, :]),
                             (idx_s[:, :], src_sh), (dst_s[:, :], dst_sh)]
                else:
                    pairs = [(idx[:, g:g + 3, :], src_g[:, bass.ds(k0, 3), :]), (dst_i[:, g:g + 3, :], dst_gr[:, bass.ds(k0, 3), :])]
                for to, at in pairs:
                    sp.dma_start(to, at).then_inc(idx_in[c], 16)

            for c in range(3):
                load_chunk(0, c)
            for c in range(XC):
                sp.wait_ge(xn_ready, c + 1)
                sp.dma_start(xn_rows[:, c * TC:(c + 1) * TC, :], xbuf[:, c * TC:(c + 1) * TC, :]).then_inc(xn_out[c], 16)
            sp.wait_ge(deg_done, 1)
            sp.dma_start(deg_tab.rearrange("(p c) -> p c", c=LO), deg_hl[:, :]).then_inc(deg_out, 16)
            sp.wait_ge(deg_out, 16)
            sp.dma_start(deg[:, :], deg_tab[0:N].rearrange("(p c) -> p c", c=RT)).then_inc(deg_in, 16)
            sp.wait_ge(minmax_done, 2)
            sp.dma_start(min_tab.rearrange("(p s) -> p s", s=2), gmin[:, :]).then_inc(minmax_out, 16)
            sp.dma_start(max_tab.rearrange("(p s) -> p s", s=2), gmax[:, :]).then_inc(minmax_out, 16)
            sp.wait_ge(minmax_out, 32)
            sp.dma_start(base_i[:, :], min_tab.rearrange("(a g) -> a g", a=1)).then_inc(base_in, 16)
            sp.dma_start(max_i, max_tab.rearrange("(a g) -> a g", a=1)).then_inc(base_in, 16)
            sp.dma_start(base_bi, min_tab.rearrange("(a g) -> a g", a=1).broadcast_to([P, NG])).then_inc(base_in, 16)
            for c in range(YC):
                sp.wait_ge(y_scaled, c + 1)
                sp.dma_start(y_rows[:, c * TY:(c + 1) * TY, :], ybuf[c % YBUF]).then_inc(y_out[c % YBUF], 16)
            sp.wait_ge(r_ready, 2)
            sp.dma_start(r_tab.rearrange("(p c) -> p c", c=RT), r_small[:, :]).then_inc(r_out, 16)
            sp.wait_ge(r_out, 16)

            def load_weights():
                y_written(sp)
                for c in range(XC):
                    sp.wait_ge(xn_out[c], 16)
                sp.dma_start(w1_sb, w1.rearrange("e (k p) h -> p e k h", p=P)).then_inc(w_in, 16)
                sp.dma_start(w2_sb, w2.rearrange("e (c p) d -> p e c d", p=P)).then_inc(w_in, 16)

            def load_block(b):
                at = b * NB
                sp.dma_start(x_blk[:, :, :], x[bass.ds(at, NB), :].rearrange("(s p) d -> p s d", s=2)).then_inc(blk_in, 16)
                sp.dma_start(xn_blk[:, :, :], xn_tab[bass.ds(at, NB), :].rearrange("(s p) d -> p s d", s=2)).then_inc(blk_in, 16)
                sp.dma_start(r_blk[:, :], r_tab[bass.ds(at, NB)].rearrange("(a n) -> a n", a=1).broadcast_to([P, NB])).then_inc(blk_in, 16)

            def store_block(b):
                sp.wait_ge(y_added, 8 * b + 8)
                sp.dma_start(out[bass.ds(b * NB, NB), :].rearrange("(s p) d -> p s d", s=2), outb[:, :, :]).then_inc(stored, 16)

            def iteration(j, edges, new, old):
                if edges:
                    sp.wait_ge(summed, GPI * j + 3)
                    load_chunk(j + 1, 0)
                    if isinstance(j, int) and j == 0:
                        load_weights()
                if new:
                    sp.wait_ge(x1_done, j)
                if not (isinstance(j, int) and j >= NBLK):
                    load_block(j)
                if edges:
                    sp.wait_ge(summed, GPI * j + 6)
                    load_chunk(j + 1, 1)
                if old:
                    store_block(j - 2)
                if edges:
                    sp.wait_ge(summed, GPI * j + 9)
                    load_chunk(j + 1, 2)

            fast = path_flag(sp)
            with sp.If(fast == 1):
                iteration(0, True, False, False)
                iteration(1, True, True, False)
                with sp.Fori(2, LASTJ - 1) as j:
                    iteration(j, True, True, True)
                iteration(LASTJ - 1, True, True, True)
                iteration(LASTJ, False, True, True)
                iteration(NBLK, False, True, True)
                store_block(NBLK - 1)
            with sp.Else():
                load_weights()
                for c in range(3):
                    sp.wait_ge(idx_in[c], 32)
                with sp.Fori(0, FULL) as g:
                    sp.wait_ge(gen_acc, NBLK * g + ADD_INIT)
                    sp.dma_start(idx[:, 0:1, :], src_g[:, bass.ds(g, 1), :]).then_inc(gen_idx, 16)
                    sp.dma_start(dst_i[:, 0:1, :], dst_gr[:, bass.ds(g, 1), :]).then_inc(gen_idx, 16)
                sp.wait_ge(gen_acc, NBLK * FULL + ADD_INIT)
                sp.dma_start(idx_s[:, :], src_sh).then_inc(gen_idx, 16)
                sp.dma_start(dst_s[:, :], dst_sh).then_inc(gen_idx, 16)
                load_block(0)
                iteration(1, False, True, False)
                with sp.Fori(2, NBLK) as j:
                    iteration(j, False, True, True)
                iteration(NBLK, False, True, True)
                store_block(NBLK - 1)
            sp.wait_ge(stored, 16 * NBLK)

        @block.gpsimd
        def _(pool):
            nc.gpsimd.iota(iota_v, pattern=[[1, HI], [0, HC_COLS]], base=0, channel_multiplier=0,
                           allow_small_or_imprecise_dtypes=True).then_inc(pool_const, 1)
            nc.gpsimd.memset(zeros[:, :], 0.0).then_inc(pool_const, 1)
            nc.gpsimd.memset(eps_t[:, :], EPS).then_inc(pool_const, 1)
            nc.gpsimd.memset(ident[:, :], 0.0).then_inc(pool_const, 1)
            pool.wait_ge(pool_const, 4)
            nc.gpsimd.affine_select(out=ident[:, :], in_=ident[:, :], compare_op=ALU.not_equal, fill=1.0, base=0,
                                    pattern=[[-1, P]], channel_multiplier=1).then_inc(pool_const, 1)
            nc.gpsimd.memset(ones[:, :], 1.0).then_inc(pool_const, 1)
            for to, pat in ((iota_w[:, :], [[1, WIN]]), (iota_8[:, :], [[1, E]]), (iota_nb[:, :], [[1, NB]]),
                            (blk0[:, :], [[NB, NBLK]])):
                nc.gpsimd.iota(to, pattern=pat, base=0, channel_multiplier=0,
                               allow_small_or_imprecise_dtypes=True).then_inc(pool_const, 1)
            nc.gpsimd.iota(thr[:, 0:NBLK * GPI], pattern=[[NB, NBLK], [0, GPI]], base=0, channel_multiplier=0,
                           allow_small_or_imprecise_dtypes=True).then_inc(pool_const, 1)
            pool.wait_ge(hist_done, 1)
            pool.wait_ge(minmax_done, 2)
            pool.wait_ge(ln_sq, XC)
            nc.gpsimd.memset(acc[:, :], 0.0).then_inc(acc_zero, 1)

            def gather_group(slot, k, sem_, last=False):
                tiles, rows = shape_of(k, last)
                for t in range(tiles):
                    ix = idx_s[:, t:t + 1] if tiles != TPG else idx[:, k, t:t + 1]
                    pool.indirect_dma_start(out=ring16[0:rows, slot, t, :], out_offset=None, in_=y_tab[:, :],
                                            in_offset=bass.IndirectOffsetOnAxis(ap=ix, axis=0)).then_inc(sem_, 16)

            def iteration(j, ks):
                for k in ks:
                    if k % 3 == 0:
                        pool.wait_ge(idx_in[k // 3], 32 * (j + 1) + (32 if isinstance(j, int) and j == LASTJ and k + 2 >= LASTK else 0))
                    if known(j * GPI + k - RING + 1, 1):
                        pool.wait_ge(summed, j * GPI + k - RING + 1)
                        settle(pool)
                    gather_group(k % RING, k, gathered[k % RING], isinstance(j, int) and j == LASTJ)

            y_written(pool)
            fast = path_flag(pool)
            with pool.If(fast == 1):
                iteration(0, range(GPI))
                with pool.Fori(1, LASTJ) as j:
                    iteration(j, range(GPI))
                iteration(LASTJ, range(LASTK + 1))
            with pool.Else():
                with pool.Fori(0, FULL) as g:
                    pool.wait_ge(gen_idx, 32 * g + 32)
                    settle(pool)
                    gather_group(0, 0, gen_rows)
                pool.wait_ge(gen_idx, 32 * NG)
                gather_group(0, LASTK, gen_rows, True)

        @block.scalar
        def _(act):
            for c in range(XC):
                act.wait_ge(x_in[c], 16)
                if c:
                    act.wait_ge(ln_sum, c)
                for t in range(c * TC, (c + 1) * TC):
                    ins = nc.scalar.activation(junk_t[:, t % TC, :], xbuf[:, t, :], ACT.Copy, accum_out=rowsum[:, t:t + 1])
                ins.then_inc(ln_sum, 1)
            act.wait_ge(ln_sum, XC)
            nc.scalar.activation(negmean[:, :], rowsum[:, :], ACT.Copy, scale=-1.0 / D).then_inc(ln_neg, 1)
            act.wait_ge(ln_neg, 1)
            for t in range(RT):
                ins = nc.scalar.activation(junk_t[:, t % TC, :], xbuf[:, t, :], ACT.Square, bias=negmean[:, t:t + 1],
                                           accum_out=rowsq[:, t:t + 1])
                if t % TC == TC - 1:
                    ins.then_inc(ln_sq, 1)
                    act.wait_ge(ln_sq, t // TC + 1)
            act.wait_ge(pool_const, 4)
            nc.scalar.activation(std[:, :], rowsq[:, :], ACT.Sqrt, scale=1.0 / D, bias=eps_t[:, 0:1]).then_inc(ln_std, 1)
            act.wait_ge(ln_scale, 2)
            for t in range(RT):
                ins = nc.scalar.activation(xbuf[:, t, :], xbuf[:, t, :], ACT.Identity, scale=rstd[:, t:t + 1], bias=nmr[:, t:t + 1])
                if t % TC == TC - 1:
                    ins.then_inc(xn_ready, 1)

            def gelus(b, e):
                n = 8 * b + e
                if known(n, 2):
                    act.wait_ge(y_ready, n - 1)
                for half in range(2):
                    act.wait_ge(hid_ready, 2 * n + half + 1)
                    for c in (2 * half, 2 * half + 1):
                        ins = nc.scalar.activation(gelu[:, e % 2, c, :], ps_h[:, half, (c % 2) * NB:(c % 2 + 1) * NB],
                                                   ACT.Gelu, bias=b1_sb[:, e, c:c + 1])
                    ins.then_inc(gelu_done, 1)

            def iteration(j, new, old):
                b = j - 1
                if old:
                    gelus(b - 1, 5)
                if new:
                    act.wait_ge(emb_ready, b + 1)
                    if known(b, 1):
                        act.wait_ge(ssq_ready, b)
                    for s in range(2):
                        ins = nc.scalar.activation(junk[:, s, :], emb[:, s, :], ACT.Square, accum_out=ssq[:, s:s + 1])
                    ins.then_inc(ssq_ready, 1)
                    act.wait_ge(ssq_floor, b + 1)
                    nc.scalar.activation(rn[:, :], ssq[:, :], ACT.Sqrt).then_inc(norm_ready, 1)
                    act.wait_ge(var_ready, b + 1)
                    nc.scalar.activation(rstd2[:, :], mv[:, :, 1], ACT.Sqrt, bias=eps_t[:, 0:1]).then_inc(std2_ready, 1)
                if old:
                    gelus(b - 1, 6)
                    gelus(b - 1, 7)
                if new:
                    act.wait_ge(xn2T_done, b + 1)
                    nc.scalar.activation(xn2T[:, :, :], xnT_ps, ACT.Copy).then_inc(xn2T_ready, 1)
                    gelus(b, 0)
                    act.wait_ge(maskT_done, b + 1)
                    nc.scalar.activation(maskT[:, :, :], maskT_ps, ACT.Copy).then_inc(maskT_ready, 1)
                    for e in range(1, 5):
                        gelus(b, e)

            act.wait_ge(deg_in, 16)
            nc.scalar.activation(deg[:, :], deg[:, :], ACT.Sqrt, scale=1.0 / YSCALE ** 2).then_inc(deg_root, 1)
            act.wait_ge(r_ready, 1)
            for t in range(RT):
                n = t // TY
                if t % TY == 0 and n >= YBUF:
                    act.wait_ge(y_out[n % YBUF], 16 * (n // YBUF))
                ins = nc.scalar.activation(ybuf[n % YBUF][:, t % TY, 0:D], xbuf[:, t, :], ACT.Copy, scale=r_col[:, t:t + 1])
                if t % TY == TY - 1:
                    ins.then_inc(y_high, 1)
            act.wait_ge(const_in, 16 * 7)
            iteration(1, True, False)
            with act.Fori(2, NBLK + 1) as j:
                iteration(j, True, True)
            iteration(NBLK + 1, False, True)

        @block.tensor
        def _(pe):
            pe.wait_ge(pool_const, 2)
            nc.tensor.matmul(hist, zeros[0:SUB, 0:HI], zeros[0:SUB, 0:LO], start=True, stop=False)
            with pe.Fori(0, HCOL // (2 * HC_COLS)) as i:
                for b in range(2):
                    pe.wait_ge(hist_oh, 2 * i + b + 1)
                    for c in range(HC_COLS):
                        ins = nc.tensor.matmul(hist, oh_hi[:, b, :, c], oh_lo[:, b, :, c], start=False, stop=False)
                    ins.then_inc(hist_used, 1)
            nc.tensor.matmul(hist, zeros[0:SUB, 0:HI], zeros[0:SUB, 0:LO], start=False, stop=True).then_inc(hist_done, 1)
            pe.wait_ge(const_in, 16 * 7)
            pe.wait_ge(pool_const, 11)
            pe.wait_ge(deg_done, 1)

            def sum_group(j, k, last=False):
                g = GPI * j + k
                tiles, rows = shape_of(k, last)
                pe.wait_ge(onehot, g + 1)
                pe.wait_ge(gathered[k % RING], 16 * TPG * (3 * j + k // RING) + 16 * tiles)
                if known(g - RING + 1, 1):
                    pe.wait_ge(added, g - RING + 1)
                for h in range(KC):
                    for t in range(tiles):
                        for part in range(2):
                            at = part * D + h * P
                            nc.tensor.matmul(ps_g[:, k % RING, h * WIN:(h + 1) * WIN], ring16[0:rows, k % RING, t, at:at + P],
                                             oh[0:rows, k % RING, t, :], start=t + part == 0, stop=t + part == tiles)
                for t in range(tiles):
                    ins = nc.tensor.matmul(ps_g[:, k % RING, KC * WIN:(KC + 1) * WIN], ones[0:rows, :],
                                           oh[0:rows, k % RING, t, :], start=t == 0, stop=t == tiles - 1)
                ins.then_inc(summed, 1)

            def hidden(b, e):
                n = 8 * b + e
                if e == 0:
                    pe.wait_ge(xn2T_ready, b + 1)
                for half in range(2):
                    if known(n, 1):
                        pe.wait_ge(gelu_done, 2 * n + half - 1)
                    for c in (2 * half, 2 * half + 1):
                        for k in range(KC):
                            ins = nc.tensor.matmul(ps_h[:, half, (c % 2) * NB:(c % 2 + 1) * NB],
                                                   w1_sb[:, e, k, c * P:(c + 1) * P], xn2T[:, k, :],
                                                   start=k == 0, stop=k == KC - 1)
                    ins.then_inc(hid_ready, 1)

            def output(b, e):
                n = 8 * b + e
                pe.wait_ge(gelu_done, 2 * n + 2)
                if known(n, 2):
                    pe.wait_ge(y_added, n - 1)
                for s in range(2):
                    for c in range(HCH):
                        ins = nc.tensor.matmul(ps_y[0:SUB, e % 2, s * D:(s + 1) * D], gelu[:, e % 2, c, s * SUB:(s + 1) * SUB],
                                               w2_sb[:, e, c, :], start=c == 0, stop=c == HCH - 1)
                ins.then_inc(y_ready, 1)

            def transpose_block(rows, done):
                for s in range(2):
                    for k in range(KC):
                        ins = nc.tensor.transpose(xnT_ps[:, k, s * SUB:(s + 1) * SUB], rows[:, s, k * P:(k + 1) * P],
                                                  ident[0:SUB, 0:SUB])
                ins.then_inc(done, 1)

            def iteration(j, ks, new, old, last=False):
                b = j - 1

                def grp(k):
                    if k in ks:
                        sum_group(j, k, last)
                grp(0)
                if new:
                    pe.wait_ge(blk_in, 48 * (b + 1))
                    if known(b, 1):
                        pe.wait_ge(init_done, b)
                    transpose_block(xn_blk, xnT_ready)
                grp(1)
                if old:
                    hidden(b - 1, 5)
                    output(b - 1, 4)
                if new:
                    pe.wait_ge(uv_ready, b + 1)
                    for s in range(2):
                        for m, t in enumerate((u_t, v_t)):
                            for k in range(KC):
                                ins = nc.tensor.matmul(z_ps[:, s, :], t[:, k, s * SUB:(s + 1) * SUB], gw_sb[:, m, k, :],
                                                       start=m + k == 0, stop=m + k == KC)
                    ins.then_inc(z_ready, 1)
                grp(2)
                if old:
                    hidden(b - 1, 6)
                    output(b - 1, 5)
                grp(3)
                if old:
                    hidden(b - 1, 7)
                    output(b - 1, 6)
                if new:
                    pe.wait_ge(xn2_ready, b + 1)
                    transpose_block(emb, xn2T_done)
                if old:
                    output(b - 1, 7)
                grp(4)
                if new:
                    pe.wait_ge(xn2T_ready, b + 1)
                    for s in range(2):
                        for k in range(KC):
                            ins = nc.tensor.matmul(gate_ps[:, s, :], xn2T[:, k, s * SUB:(s + 1) * SUB], wg_sb[:, k, :],
                                                   start=k == 0, stop=k == KC - 1)
                    ins.then_inc(gate_done, 1)
                    hidden(b, 0)
                    pe.wait_ge(mask_ready, b + 1)
                    for s in range(2):
                        ins = nc.tensor.transpose(maskT_ps[:, s, :], mask[:, s, :], ident[0:SUB, 0:SUB])
                    ins.then_inc(maskT_done, 1)
                grp(5)
                if new:
                    pe.wait_ge(maskT_ready, b + 1)
                    for s in range(2):
                        ins = nc.tensor.matmul(z_ps[:, s, :], maskT[:, s, :], b2_sb[:, :], start=True, stop=True)
                    ins.then_inc(b2_done, 1)
                    hidden(b, 1)
                    output(b, 0)
                for k, e in ((6, 2), (7, 3), (8, 4)):
                    grp(k)
                    if new:
                        hidden(b, e)
                        output(b, e - 1)

            fast = path_flag(pe)
            with pe.If(fast == 1):
                iteration(0, range(GPI), False, False)
                pe.wait_ge(w_in, 32)
                iteration(1, range(GPI), True, False)
                with pe.Fori(2, LASTJ) as j:
                    iteration(j, range(GPI), True, True)
                iteration(LASTJ, range(LASTK + 1), True, True, last=True)
                iteration(NBLK, (), True, True)
                iteration(NBLK + 1, (), False, True)
            with pe.Else():
                def windows(g, tiles, rows):
                    with pe.Fori(0, NBLK) as w:
                        pe.wait_ge(gen_oh, NBLK * g + w + 1)
                        pe.wait_ge(gen_acc, NBLK * g + w + ADD_INIT)
                        for h in range(KC):
                            for t in range(tiles):
                                for part in range(2):
                                    at = part * D + h * P
                                    nc.tensor.matmul(ps_g[:, h, 0:NB], ring16[0:rows, 0, t, at:at + P], gen_hot[0:rows, t, :],
                                                     start=t + part == 0, stop=t + part == tiles)
                        for t in range(tiles):
                            ins = nc.tensor.matmul(ps_g[:, KC, 0:NB], ones[0:rows, :], gen_hot[0:rows, t, :],
                                                   start=t == 0, stop=t == tiles - 1)
                        ins.then_inc(gen_sum, 1)
                with pe.Fori(0, FULL) as g:
                    pe.wait_ge(gen_rows, 16 * TPG * g + 16 * TPG)
                    settle(pe)
                    windows(g, TPG, P)
                pe.wait_ge(gen_rows, 16 * TPG * FULL + 16 * SHORT_TILES)
                windows(FULL, SHORT_TILES, SHORT)
                pe.wait_ge(w_in, 32)
                iteration(1, (), True, False)
                with pe.Fori(2, NBLK + 1) as j:
                    iteration(j, (), True, True)
                iteration(NBLK + 1, (), False, True)

        @block.vector
        def _(dve):
            dve.wait_ge(src_in, 16)
            nc.vector.tensor_scalar(hi_i, src_i, 6, None, ALU.logical_shift_right).then_inc(hist_prep, 1)
            nc.vector.tensor_scalar(lo_i, src_i, LO - 1, None, ALU.bitwise_and).then_inc(hist_prep, 1)
            dve.wait_ge(hist_prep, 2)
            nc.vector.tensor_copy(hi_b, hi_i).then_inc(hist_prep, 1)
            nc.vector.tensor_copy(lo_b, lo_i).then_inc(hist_prep, 1)
            dve.wait_ge(hist_prep, 4)
            dve.wait_ge(pool_const, 1)

            def hot(col, b):
                for to, n, val in ((oh_hi, HI, hi_b), (oh_lo, LO, lo_b)):
                    v = val[:, bass.ds(col, HC_COLS)].rearrange("p (a c) -> p a c", a=1).broadcast_to([SUB, n, HC_COLS])
                    ins = nc.vector.tensor_tensor(to[:, b, :, :], iota_v[:, 0:n, :], v, ALU.is_equal)
                ins.then_inc(hist_oh, 1)

            HALF = HCOL // (2 * HC_COLS) // 2
            hot(0, 0)
            hot(HC_COLS, 1)
            with dve.Fori(1, HALF) as i:
                for b in range(2):
                    dve.wait_ge(hist_used, 2 * i + b - 1)
                    hot(i * 2 * HC_COLS + b * HC_COLS, b)
            dve.wait_ge(ln_std, 1)
            nc.vector.reciprocal(rstd[:, :], std[:, :]).then_inc(ln_scale, 1)
            dve.wait_ge(ln_scale, 1)
            nc.vector.tensor_tensor(nmr[:, :], negmean[:, :], rstd[:, :], ALU.mult).then_inc(ln_scale, 1)
            with dve.Fori(HALF, HCOL // (2 * HC_COLS)) as i:
                for b in range(2):
                    dve.wait_ge(hist_used, 2 * i + b - 1)
                    hot(i * 2 * HC_COLS + b * HC_COLS, b)
            dve.wait_ge(hist_done, 1)
            nc.vector.tensor_scalar(deg_hl[:, :], hist, 1.0, None, ALU.max).then_inc(deg_done, 1)
            dve.wait_ge(dst_in, 48)
            nc.vector.tensor_reduce(gmin[:, :], dst_g, AX.X, ALU.min).then_inc(minmax_done, 1)
            nc.vector.tensor_reduce(gmax[:, :], dst_g, AX.X, ALU.max).then_inc(minmax_done, 1)
            dve.wait_ge(deg_root, 1)
            nc.vector.reciprocal(r_col[:, :], deg[:, :]).then_inc(r_ready, 1)
            dve.wait_ge(r_ready, 1)
            nc.vector.tensor_scalar(r_small[:, :], r_col[:, :], YSCALE ** -2, None, ALU.mult).then_inc(r_ready, 1)
            for t in range(RT):
                n = t // TY
                if t % TY == 0:
                    dve.wait_ge(y_high, n + 1)
                ins = nc.vector.scalar_tensor_tensor(out=ybuf[n % YBUF][:, t % TY, D:2 * D], in0=xbuf[:, t, :],
                                                     scalar=r_col[:, t:t + 1], in1=ybuf[n % YBUF][:, t % TY, 0:D],
                                                     op0=ALU.mult, op1=ALU.subtract)
                if t % TY == TY - 1:
                    ins.then_inc(y_scaled, 1)
            dve.wait_ge(base_in, 48)
            dve.wait_ge(pool_const, 11)
            link = steps(dve, flag_chain, 0)
            link(nc.vector.tensor_copy(base_f[:, :], base_bi))
            link(nc.vector.tensor_tensor(span, max_i, base_f[0:1, :], ALU.subtract))
            link(nc.vector.memset(late, 0.0))
            link(nc.vector.tensor_tensor(late[:, LEAD:NG], thr[:, 0:NG - LEAD], base_f[0:1, LEAD:NG], ALU.subtract))
            link(nc.vector.tensor_reduce(flag_f[:, 0:1], span, AX.X, ALU.max))
            link(nc.vector.tensor_reduce(flag_f[:, 1:2], late, AX.X, ALU.max))
            link(nc.vector.tensor_scalar(flag_f[:, 0:1], flag_f[:, 0:1], float(WIN - 1), None, ALU.is_le))
            link(nc.vector.tensor_scalar(flag_f[:, 1:2], flag_f[:, 1:2], 0.0, None, ALU.is_le))
            nc.vector.tensor_tensor(flag[:, :], flag_f[:, 0:1], flag_f[:, 1:2], ALU.mult).then_inc(flag_ready, 1)
            dve.wait_ge(const_in, 16 * 7)
            dve.wait_ge(acc_zero, 1)

            def hot_group(j, k, last=False):
                g = GPI * j + k
                tiles, rows = shape_of(k, last)
                extra = 32 if isinstance(j, int) and j == LASTJ and 3 * (k // 3) + 2 >= LASTK else 0
                dve.wait_ge(idx_in[k // 3], 32 * (j + 1) + extra)
                if known(g - RING + 1, 1):
                    dve.wait_ge(summed, g - RING + 1)
                d = dst_s[:, :] if tiles != TPG else dst_i[:, k, :]
                base = base_f[0:rows, bass.ds(g, 1)].broadcast_to([rows, tiles])
                nc.vector.tensor_tensor(loc[0:rows, k % RING, 0:tiles], d, base, ALU.subtract).then_inc(loc_ready, 1)
                dve.wait_ge(loc_ready, g + 1)
                iw = iota_w[0:rows, :].rearrange("p (a w) -> p a w", a=1).broadcast_to([rows, tiles, WIN])
                lc = loc[0:rows, k % RING, 0:tiles].rearrange("p (t a) -> p t a", a=1).broadcast_to([rows, tiles, WIN])
                nc.vector.tensor_tensor(oh[0:rows, k % RING, 0:tiles, :], iw, lc, ALU.is_equal).then_inc(onehot, 1)

            def add_group(j, k):
                g = GPI * j + k
                first = dve.value_load(base_i[0:1, bass.ds(g, 1)], min_val=0, max_val=N - 1)
                dve.wait_ge(summed, g + 1)
                if known(g, 1):
                    dve.wait_ge(added, g)
                to = acc3[:, :, bass.ds(first, WIN)]
                fr = ps_g[:, k % RING, 0:3 * WIN].rearrange("p (c w) -> p c w", c=3)
                nc.vector.tensor_tensor(to, to, fr, ALU.add).then_inc(added, 1)

            def add_expert(b, e):
                n = 8 * b + e
                dve.wait_ge(y_ready, n + 1)
                if e == 0:
                    dve.wait_ge(init_done, b + 1)
                else:
                    dve.wait_ge(y_added, n)
                to = outb if e == E - 1 else accy
                if e == E - 1 and known(b, 1):
                    dve.wait_ge(stored, 16 * b)
                for s in range(2):
                    ins = nc.vector.scalar_tensor_tensor(out=to[:, s, :], in0=ps_y[0:SUB, e % 2, s * D:(s + 1) * D],
                                                         scalar=mask[:, s, e:e + 1], in1=accy[:, s, :],
                                                         op0=ALU.mult, op1=ALU.add)
                ins.then_inc(y_added, 1)

            def iteration(j, ks, new, old, last=False, general=False):
                b = j - 1

                def grp(k):
                    if k in ks:
                        add_group(j, k)
                        nk = k + 2
                        if nk < GPI:
                            if not last or nk <= LASTK:
                                hot_group(j, nk, last)
                        elif not last:
                            hot_group(j + 1, nk - GPI)
                grp(0)
                grp(1)
                if new:
                    link = steps(dve, uv_chain, 3 * b)
                    dve.wait_ge(blk_in, 48 * (b + 1))
                    dve.wait_ge(xnT_ready, b + 1)
                    if known(b, 1):
                        dve.wait_ge(z_ready, b)
                    if general:
                        dve.wait_ge(gen_acc, NBLK * NG + ADD_INIT)
                    else:
                        dve.wait_ge(added, GPI * j + LEAD if ks else NG)
                    s_t = acc3[:, 0:KC, bass.ds(b * NB, NB)]
                    cnt = acc3[:, KC:KC + 1, bass.ds(b * NB, NB)].broadcast_to([P, KC, NB])
                    rb = r_blk[:, :].rearrange("p (a n) -> p a n", a=1).broadcast_to([P, KC, NB])
                    link(nc.vector.tensor_tensor(rs[:, :, :], s_t, rb, ALU.mult))
                    link(nc.vector.tensor_tensor(v_t[:, :, :], rs[:, :, :], xnT_ps, ALU.mult))
                    link(nc.vector.tensor_tensor(u_t[:, :, :], rs[:, :, :], xnT_ps, ALU.add))
                    nc.vector.scalar_tensor_tensor(out=u_t[:, :, :], in0=cnt, scalar=0.0, in1=u_t[:, :, :],
                                                   op0=ALU.is_gt, op1=ALU.mult).then_inc(uv_ready, 1)
                if old:
                    add_expert(b - 1, 4)
                if new:
                    link = steps(dve, z_chain, 6 * b)
                    dve.wait_ge(z_ready, b + 1)
                    bias = gb_b[:, :].rearrange("p (a d) -> p a d", a=1).broadcast_to([SUB, 2, D])
                    if known(b, 1):
                        dve.wait_ge(xn2T_done, b)
                    link(nc.vector.tensor_tensor(emb[:, :, :], z_ps, bias, ALU.add))
                    nc.vector.scalar_tensor_tensor(out=emb[:, :, :], in0=emb[:, :, :], scalar=0.01, in1=emb[:, :, :],
                                                   op0=ALU.mult, op1=ALU.max).then_inc(emb_ready, 1)
                    dve.wait_ge(emb_ready, b + 1)
                    dve.wait_ge(ssq_ready, b + 1)
                    nc.vector.tensor_scalar(ssq[:, :], ssq[:, :], 1e-24, None, ALU.max).then_inc(ssq_floor, 1)
                    dve.wait_ge(norm_ready, b + 1)
                    link(nc.vector.reciprocal(rn[:, :], rn[:, :]))
                    for s in range(2):
                        ins = nc.vector.scalar_tensor_tensor(out=x1[:, s, :], in0=emb[:, s, :], scalar=rn[:, s:s + 1],
                                                             in1=x_blk[:, s, :], op0=ALU.mult, op1=ALU.add)
                        if s == 0:
                            link(ins)
                    ins.then_inc(x1_done, 1)
                    dve.wait_ge(x1_done, b + 1)
                    for s in range(2):
                        link(nc.vector.bn_stats(stats[:, s, :], x1[:, s, :]), settle)
                    for s in range(2):
                        ins = nc.vector.bn_aggr(mv[:, s, :], stats[:, s, :])
                    ins.then_inc(var_ready, 1)
                    dve.wait_ge(std2_ready, b + 1)
                    link(nc.vector.reciprocal(rstd2[:, :], rstd2[:, :]))
                    for s in range(2):
                        ins = nc.vector.tensor_scalar(emb[:, s, :], x1[:, s, :], mv[:, s, 0:1], rstd2[:, s:s + 1],
                                                      ALU.subtract, ALU.mult)
                    ins.then_inc(xn2_ready, 1)
                    assert link.at[0] == 6
                grp(2)
                if old:
                    add_expert(b - 1, 5)
                grp(3)
                if old:
                    add_expert(b - 1, 6)
                    add_expert(b - 1, 7)
                grp(4)
                if new:
                    link = steps(dve, gate_chain, 9 * b)
                    dve.wait_ge(gate_done, b + 1)
                    bias = bg_b[:, :].rearrange("p (a e) -> p a e", a=1).broadcast_to([SUB, 2, E])
                    link(nc.vector.tensor_tensor(score[:, :, :], gate_ps, bias, ALU.add), settle)
                    for s in range(2):
                        link(nc.vector.max(top[:, s, :], score[:, s, :]), settle)
                    for s in range(2):
                        link(nc.vector.max_index(topi[:, s, :], top[:, s, :], score[:, s, :]), settle)
                    link(nc.vector.tensor_copy(topf[:, :, :], topi[:, :, :]))
                    for s in range(2):
                        link(nc.vector.tensor_scalar(mask[:, s, :], iota_8[:, :], topf[:, s, 0:1], None, ALU.is_equal))
                        ins = nc.vector.scalar_tensor_tensor(out=mask[:, s, :], in0=iota_8[:, :], scalar=topf[:, s, 1:2],
                                                             in1=mask[:, s, :], op0=ALU.is_equal, op1=ALU.add)
                        if s == 0:
                            link(ins)
                    ins.then_inc(mask_ready, 1)
                    assert link.at[0] == 9
                    dve.wait_ge(mask_ready, b + 1)
                grp(5)
                if new:
                    dve.wait_ge(b2_done, b + 1)
                    if known(b, 1):
                        dve.wait_ge(y_added, 8 * b)
                    nc.vector.tensor_tensor(accy[:, :, :], x1[:, :, :], z_ps, ALU.add).then_inc(init_done, 1)
                    add_expert(b, 0)
                for k, e in ((6, 1), (7, 2), (8, 3)):
                    grp(k)
                    if new:
                        add_expert(b, e)

            fast = path_flag(dve)
            with dve.If(fast == 1):
                hot_group(0, 0)
                hot_group(0, 1)
                iteration(0, range(GPI), False, False)
                iteration(1, range(GPI), True, False)
                with dve.Fori(2, LASTJ) as j:
                    iteration(j, range(GPI), True, True)
                iteration(LASTJ, range(LASTK + 1), True, True, last=True)
                iteration(NBLK, (), True, True)
                iteration(NBLK + 1, (), False, True)
            with dve.Else():
                nc.vector.memset(loc[:, 1, :], 0.0).then_inc(gen_acc, ADD_INIT)

                def windows(g, d, tiles, rows):
                    with dve.Fori(0, NBLK) as w:
                        dve.wait_ge(gen_acc, NBLK * g + w + ADD_INIT)
                        first = blk0[0:rows, bass.ds(w, 1)].broadcast_to([rows, tiles])
                        nc.vector.tensor_tensor(loc[0:rows, 0, 0:tiles], d, first, ALU.subtract).then_inc(gen_loc, 1)
                        dve.wait_ge(gen_loc, NBLK * g + w + 1)
                        it = iota_nb[0:rows, :].rearrange("p (a w) -> p a w", a=1).broadcast_to([rows, tiles, NB])
                        lc = loc[0:rows, 0, 0:tiles].rearrange("p (t a) -> p t a", a=1).broadcast_to([rows, tiles, NB])
                        nc.vector.tensor_tensor(gen_hot[0:rows, 0:tiles, :], it, lc, ALU.is_equal).then_inc(gen_oh, 1)
                        dve.wait_ge(gen_sum, NBLK * g + w + 1)
                        to = acc3[:, :, bass.ds(w * NB, NB)]
                        nc.vector.tensor_tensor(to, to, ps_g[:, :, 0:NB], ALU.add).then_inc(gen_acc, 1)
                with dve.Fori(0, FULL) as g:
                    dve.wait_ge(gen_idx, 32 * g + 32)
                    settle(dve)
                    windows(g, dst_i[:, 0, :], TPG, P)
                dve.wait_ge(gen_idx, 32 * NG)
                windows(FULL, dst_s[:, :], SHORT_TILES, SHORT)
                iteration(1, (), True, False, general=True)
                with dve.Fori(2, NBLK + 1) as j:
                    iteration(j, (), True, True, general=True)
                iteration(NBLK + 1, (), False, True, general=True)


_INS = ['x', 'src', 'dst', 'L0_gnn_W1', 'L0_gnn_W2', 'L0_gnn_b', 'L0_ffn_Wg', 'L0_ffn_bg', 'L0_ffn_W1', 'L0_ffn_b1',
        'L0_ffn_W2', 'L0_ffn_b2']


def kernel(**inputs):
    import numpy as _np
    import concourse.bacc as _bacc
    from concourse import mybir as _mybir
    from concourse.bass_utils import run_bass_kernel_spmd as _run

    nc = _bacc.Bacc("TRN2", target_bir_lowering=False, num_devices=1)
    arrays, args = {}, []
    for name in _INS:
        a = _np.ascontiguousarray(inputs[name])
        if name == 'src':
            a = a.view(_np.uint32)
        if name == 'L0_ffn_b1':
            a = _np.ascontiguousarray(a.reshape(a.shape[0], -1, 128).transpose(2, 0, 1))
        arrays[f"in_{name}"] = a
        args.append(nc.dram_tensor(f"in_{name}", a.shape, _mybir.dt.from_np(a.dtype), kind="ExternalInput").ap())
    shape = inputs['x'].shape
    args.append(nc.dram_tensor("out_0", shape, _mybir.dt.float32, kind="ExternalOutput").ap())
    bass_gnn_ffn(nc, *args)
    r = _run(nc, [arrays], core_ids=[0])
    return r.results[0]["out_0"]
```

```python
from contextlib import ExitStack

import concourse.bass as bass
from concourse import mybir

F32 = mybir.dt.float32
BF16 = mybir.dt.bfloat16
F16 = mybir.dt.float16
I32 = mybir.dt.int32
U32 = mybir.dt.uint32
ALU = mybir.AluOpType
ACT = mybir.ActivationFunctionType
AX = mybir.AxisListType

P = 128
EPS = 1e-5
TPG = 7
GE = TPG * P
GPI = 9
RING = 3
WIN = 64
NB = 250
SUB = 125
SPLIT = 5
LEAD = 1
HC_COLS = 32
WSCALE = 1024.0
W_SQUARES = 16.0
B_SQUARES = 4096.0
XSCALE = 64.0
YSCALE = 64.0


def steps(eng, sem, base):
    at = [0]

    def link(ins, after=None):
        at[0] += 1
        ins.then_inc(sem, 1)
        eng.wait_ge(sem, base + at[0])
        if after:
            after(eng)
    link.at = at
    return link


def bass_gnn_ffn(nc, x, src, dst, gw1, gw2, gb, wg, bg, w1, b1, w2, b2, out):
    N, D = x.shape
    NE = src.shape[0]
    E, _, H = w1.shape
    KC = D // P
    HCH = H // P
    NBLK = N // NB
    FULL = NE // GE
    NG = FULL + 1
    SHORT_TILES = 2
    SHORT = (NE - FULL * GE) // SHORT_TILES
    LASTJ = (NG - 1) // GPI
    LASTK = (NG - 1) % GPI
    ACCW = N + WIN
    RT = N // SUB
    XC = 5
    TC = RT // XC
    YC = 10
    TY = RT // YC
    YBUF = 4
    HCOL = NE // SUB
    LO = 64
    HI = -(-N // LO)
    MG = NG // 2
    assert NBLK * NB == N and NG % 2 == 0 and KC == 2 and SHORT * SHORT_TILES + FULL * GE == NE and SHORT <= P
    assert LASTJ == NBLK - 1 and HCOL % (2 * HC_COLS) == 0 and RT * SUB == N

    y_tab = nc.dram_tensor("y_tab", (N, 2 * D), F16, kind="Internal").ap()
    xn_tab = nc.dram_tensor("xn_tab", (N, D), F32, kind="Internal").ap()
    deg_tab = nc.dram_tensor("deg_tab", (HI * LO,), F32, kind="Internal").ap()
    r_tab = nc.dram_tensor("r_tab", (N,), F32, kind="Internal").ap()
    min_tab = nc.dram_tensor("min_tab", (NG,), I32, kind="Internal").ap()
    max_tab = nc.dram_tensor("max_tab", (NG,), I32, kind="Internal").ap()

    with ExitStack() as ctx:
        def sb(name, shape, dt=F32):
            return ctx.enter_context(nc.sbuf_tensor(name, shape, dt))

        def psum(name, shape):
            return ctx.enter_context(nc.psum_tensor(name, shape, F32))

        def sem(name):
            return ctx.enter_context(nc.semaphore(name))

        acc = sb("acc", [P, 3 * ACCW])
        acc3 = acc[:, :].rearrange("p (c n) -> p c n", c=3)
        wts = sb("wts", [P, E * (KC * H + HCH * D)])
        w1_sb = wts[:, 0:E * KC * H].rearrange("p (e k h) -> p e k h", e=E, k=KC)
        w2_sb = wts[:, E * KC * H:].rearrange("p (e c d) -> p e c d", e=E, c=HCH)
        w1_16 = wts[:, 0:E * KC * H].bitcast(F16).rearrange("p (e a k h) -> p e a k h", e=E, a=2, k=KC)
        w2_16 = wts[:, E * KC * H:].bitcast(F16).rearrange("p (e a c d) -> p e a c d", e=E, a=2, c=HCH)
        ring = sb("ring", [P, RING, TPG, D])
        ring16 = ring[:, :, :, :].bitcast(F16)
        idx = sb("idx", [P, GPI, TPG], U32)
        dst_i = sb("dst_i", [P, GPI, TPG], I32)
        idx_s = sb("idx_s", [SHORT, SHORT_TILES], U32)
        dst_s = sb("dst_s", [SHORT, SHORT_TILES], I32)
        loc = sb("loc", [P, RING, TPG])
        oh = sb("oh", [P, RING, TPG, WIN], F16)
        gw_sb = sb("gw_sb", [P, 2, KC, D])
        gb_b = sb("gb_b", [SUB, D])
        wg_sb = sb("wg_sb", [P, KC, E])
        bg_b = sb("bg_b", [SUB, E])
        b1_sb = sb("b1_sb", [P, E, HCH])
        b2_sb = sb("b2_sb", [E, D])
        x_blk = sb("x_blk", [SUB, 2, D])
        xn_blk = sb("xn_blk", [SUB, 2, D])
        r_blk = sb("r_blk", [P, NB])
        u_t = sb("u_t", [P, KC, NB])
        v_t = sb("v_t", [P, KC, NB])
        emb = sb("emb", [SUB, 2, D])
        junk = sb("junk", [SUB, 2, D], BF16)
        x1 = sb("x1", [SUB, 2, D])
        xn2T = sb("xn2T", [P, KC, NB])
        xn2_16 = sb("xn2_16", [P, 2, KC, NB], F16)
        hid = sb("hid", [P, 2, KC * H])
        gelu = hid[:, :, 0:HCH * NB].rearrange("p b (c n) -> p b c n", c=HCH)
        gelu16 = hid[:, :, 0:HCH * NB].bitcast(F16).rearrange("p b (a c n) -> p b a c n", a=2, c=HCH)
        gelu_f = sb("gelu_f", [P, HCH, NB])
        accy = sb("accy", [SUB, 2, D])
        outb = sb("outb", [SUB, 2, D])
        ssq = sb("ssq", [SUB, 2])
        rn = sb("rn", [SUB, 2])
        stats = sb("stats", [SUB, 2, 6])
        mv = sb("mv", [SUB, 2, 2])
        rstd2 = sb("rstd2", [SUB, 2])
        score = sb("score", [SUB, 2, E])
        top = sb("top", [SUB, 2, 8])
        topi = sb("topi", [SUB, 2, 8], U32)
        topf = sb("topf", [SUB, 2, 8])
        mask = sb("mask", [SUB, 2, E])
        mask_s = sb("mask_s", [SUB, 2, E])
        maskT = sb("maskT", [E, 2, SUB])
        ident = sb("ident", [P, P])
        iota_nb = sb("iota_nb", [P, NB])
        iota_w = iota_nb[:, 0:WIN]
        iota_8 = iota_nb[0:SUB, 0:E]
        blk0 = sb("blk0", [P, NBLK])
        ones = sb("ones", [P, P], F16)
        zeros = sb("zeros", [P, P], BF16)
        base_i = sb("base_i", [1, NG], I32)
        base_f = sb("base_f", [P, NG])
        flag_f = sb("flag_f", [1, 4])
        flag = sb("flag", [1, 1], I32)
        xbuf = wts[0:SUB, 0:RT * D].rearrange("p (t d) -> p t d", d=D)
        hi_b = wts[0:SUB, RT * D:RT * D + HCOL // 2].bitcast(BF16)
        lo_b = wts[0:SUB, RT * D + HCOL // 2:RT * D + HCOL].bitcast(BF16)
        YW = TY * D
        ybuf = [wts[0:SUB, RT * D + n * YW:RT * D + (n + 1) * YW].bitcast(F16).rearrange("p (t c) -> p t c", c=2 * D)
                for n in range(2)]
        ybuf += [ring16[0:SUB, 1 + n:2 + n, 0:TY, :].rearrange("p a t c -> p (a t) c") for n in range(2)]
        ones_f = sb("ones_f", [P, 1])
        rows0 = ring[:, 0:1, :, :].rearrange("p a t d -> p (a t) d")
        r_small = rows0[0:SUB, 6, 3 * RT:4 * RT]
        squares = rows0[:, 6, 4 * RT:4 * RT + 2 * E + 1]
        base_bi = rows0[:, 0, 0:NG].bitcast(I32)
        max_i = rows0[0:1, 1, 0:NG].bitcast(I32)
        thr = rows0[0:1, 2, :]
        span = rows0[0:1, 3, 0:NG]
        late = rows0[0:1, 4, 0:NG]
        a0 = 0

        def part(n):
            nonlocal a0
            a0 += n
            return acc[:, a0 - n:a0]
        src_i = part(HCOL)[0:SUB].bitcast(U32)
        hi_i = part(HCOL)[0:SUB].bitcast(U32)
        lo_i = part(HCOL)[0:SUB].bitcast(U32)
        iota_v = part(HI * HC_COLS // 2)[0:SUB].bitcast(BF16).rearrange("p (v c) -> p v c", c=HC_COLS)
        oh_hi = part(HI * HC_COLS)[0:SUB].bitcast(BF16).rearrange("p (b v c) -> p b v c", b=2, c=HC_COLS)
        oh_lo = part(LO * HC_COLS)[0:SUB].bitcast(BF16).rearrange("p (b v c) -> p b v c", b=2, c=HC_COLS)
        junk_t = part(TC * D // 2)[0:SUB].bitcast(BF16).rearrange("p (t d) -> p t d", d=D)
        junk_w = acc[:, a0 - TC * D // 2:a0 - TC * D // 2 + KC * H].bitcast(BF16).rearrange("p (b c) -> p b c", b=2)
        w_parts = [wts[:, m * E * KC * H:(m + 1) * E * KC * H].bitcast(F16).rearrange("p (e a c) -> p e a c", e=E, a=2) for m in range(2)]
        w_raw = [w1.rearrange("e (k p) h -> e p k h", p=P), w2.rearrange("e (c p) d -> e p c d", p=P)]
        w_inner = [KC, HCH]
        dst_g = part(2 * GE)[0:MG].bitcast(I32).rearrange("p (s e) -> p s e", s=2)
        gmin = part(2)[0:MG].bitcast(I32)
        gmax = part(2)[0:MG].bitcast(I32)
        deg_hl = part(LO)[0:HI]
        deg = rows0[0:SUB, 5, 0 * RT:1 * RT]
        r_col = rows0[0:SUB, 5, 1 * RT:2 * RT]
        negmean = rows0[0:SUB, 5, 2 * RT:3 * RT]
        rowsum = rows0[0:SUB, 5, 3 * RT:4 * RT]
        rowsq = rows0[0:SUB, 5, 4 * RT:5 * RT]
        std = rows0[0:SUB, 6, 0 * RT:1 * RT]
        rstd = rows0[0:SUB, 6, 1 * RT:2 * RT]
        nmr = rows0[0:SUB, 6, 2 * RT:3 * RT]
        eps_t = sb("eps_t", [SUB, 1])

        ps_g = psum("ps_g", [P, RING, 512])
        ps_h = psum("ps_h", [P, 2, 512])
        ps_y = psum("ps_y", [P, 2, 512])
        ps_a = psum("ps_a", [P, 512])
        hist = ps_a[0:HI, 0:LO]
        xnT_ps = ps_a[:, 0:KC * NB].rearrange("p (k n) -> p k n", k=KC)
        z_ps = ps_a[0:SUB, :].rearrange("p (s d) -> p s d", s=2)
        gate_ps = ps_a[0:SUB, 0:2 * E].rearrange("p (s e) -> p s e", s=2)
        maskT_ps = ps_a[0:E, 0:NB].rearrange("p (s n) -> p s n", s=2)

        src_in = sem("src_in")
        x_in = [sem(f"x_in{c}") for c in range(XC)]
        dst_in = sem("dst_in")
        const_in = sem("const_in")
        pool_const = sem("pool_const")
        hist_prep = sem("hist_prep")
        hist_oh = sem("hist_oh")
        hist_used = sem("hist_used")
        hist_done = sem("hist_done")
        minmax_done = sem("minmax_done")
        minmax_out = sem("minmax_out")
        base_in = sem("base_in")
        flag_chain = sem("flag_chain")
        flag_ready = sem("flag_ready")
        deg_done = sem("deg_done")
        deg_out = sem("deg_out")
        deg_in = sem("deg_in")
        deg_root = sem("deg_root")
        r_ready = sem("r_ready")
        r_out = sem("r_out")
        ln_sum = sem("ln_sum")
        ln_neg = sem("ln_neg")
        ln_sq = sem("ln_sq")
        ln_std = sem("ln_std")
        ln_scale = sem("ln_scale")
        xn_ready = sem("xn_ready")
        xn_out = [sem(f"xn_out{c}") for c in range(XC)]
        y_scaled = sem("y_scaled")
        y_high = sem("y_high")
        y_out = [sem(f"y_out{n}") for n in range(YBUF)]
        acc_zero = sem("acc_zero")
        raw_in = [sem(f"raw_in{m}") for m in range(2)]
        w_high = sem("w_high")
        w_low = sem("w_low")
        squares_done = sem("squares_done")
        square_sums = sem("square_sums")
        w_in = sem("w_in")
        idx_in = [sem(f"idx_in{c}") for c in range(3)]
        gathered = [sem(f"gathered{s}") for s in range(RING)]
        loc_ready = sem("loc_ready")
        onehot = sem("onehot")
        summed = sem("summed")
        added = sem("added")
        blk_in = sem("blk_in")
        xnT_ready = sem("xnT_ready")
        uv_chain = sem("uv_chain")
        uv_ready = sem("uv_ready")
        z_ready = sem("z_ready")
        z_chain = sem("z_chain")
        emb_ready = sem("emb_ready")
        ssq_ready = sem("ssq_ready")
        ssq_floor = sem("ssq_floor")
        norm_ready = sem("norm_ready")
        var_ready = sem("var_ready")
        std2_ready = sem("std2_ready")
        x1_done = sem("x1_done")
        xn2_ready = sem("xn2_ready")
        xn2T_done = sem("xn2T_done")
        xn2T_ready = sem("xn2T_ready")
        gate_done = sem("gate_done")
        gate_chain = sem("gate_chain")
        mask_ready = sem("mask_ready")
        mask_scaled = sem("mask_scaled")
        maskT_done = sem("maskT_done")
        maskT_ready = sem("maskT_ready")
        b2_done = sem("b2_done")
        init_done = sem("init_done")
        hid_ready = sem("hid_ready")
        gelu_done = sem("gelu_done")
        gelu_raw = sem("gelu_raw")
        low_done = sem("low_done")
        x16_high = sem("x16_high")
        x16_ready = sem("x16_ready")
        y_ready = sem("y_ready")
        y_added = sem("y_added")
        stored = sem("stored")
        waited = sem("waited")
        gen_idx = sem("gen_idx")
        gen_rows = sem("gen_rows")
        gen_loc = sem("gen_loc")
        gen_oh = sem("gen_oh")
        gen_sum = sem("gen_sum")
        gen_acc = sem("gen_acc")
        gen_hot = ring16[:, 1:2, :, :].rearrange("p a t d -> p (a t) d")[:, :, 0:NB]

        def settle(eng):
            eng.sem_inc(waited, 1)

        def path_flag(eng):
            eng.wait_ge(flag_ready, 1)
            return eng.value_load(flag[0:1, 0:1], min_val=0, max_val=1)

        def y_written(eng):
            for n in range(YBUF):
                eng.wait_ge(y_out[n], 16 * len(range(n, YC, YBUF)))

        block = ctx.enter_context(nc.Block())

        x_rows = x.rearrange("(p t) d -> p t d", t=RT)
        y_rows = y_tab.rearrange("(p t) c -> p t c", t=RT)
        xn_rows = xn_tab.rearrange("(p t) d -> p t d", t=RT)
        src_g = src[0:FULL * GE].rearrange("(g p j) -> p g j", p=P, j=TPG)
        dst_gr = dst[0:FULL * GE].rearrange("(g p j) -> p g j", p=P, j=TPG)
        src_sh = src[FULL * GE:NE].rearrange("(p j) -> p j", j=SHORT_TILES)
        dst_sh = dst[FULL * GE:NE].rearrange("(p j) -> p j", j=SHORT_TILES)
        ADD_INIT = 1

        def known(v, low):
            return not isinstance(v, int) or v >= low

        def shape_of(k, last):
            return (SHORT_TILES, SHORT) if last and k == LASTK else (TPG, P)

        @block.sync
        def _(sp):
            sp.dma_start(src_i, src.rearrange("(p c) -> p c", c=HCOL)).then_inc(src_in, 16)
            for c in range(XC):
                sp.dma_start(xbuf[:, c * TC:(c + 1) * TC, :], x_rows[:, c * TC:(c + 1) * TC, :]).then_inc(x_in[c], 16)
            whole = (MG - 1) * 2 * GE
            rest = NE - whole
            dg = dst_g.rearrange("p s e -> p (s e)")
            sp.dma_start(dg[0:MG - 1, :], dst[0:whole].rearrange("(p c) -> p c", c=2 * GE)).then_inc(dst_in, 16)
            sp.dma_start(dg[MG - 1:MG, 0:rest], dst[whole:NE].rearrange("(a c) -> a c", a=1)).then_inc(dst_in, 16)
            sp.dma_start(dg[MG - 1:MG, rest:2 * GE], dst[NE - (2 * GE - rest):NE].rearrange("(a c) -> a c", a=1)).then_inc(dst_in, 16)
            sp.dma_start(gw_sb[:, 0, :, :], gw1.rearrange("(k p) d -> p k d", p=P)).then_inc(const_in, 16)
            sp.dma_start(gw_sb[:, 1, :, :], gw2.rearrange("(k p) d -> p k d", p=P)).then_inc(const_in, 16)
            sp.dma_start(gb_b[:, :], gb.rearrange("(a d) -> a d", a=1).broadcast_to([SUB, D])).then_inc(const_in, 16)
            sp.dma_start(wg_sb[:, :, :], wg.rearrange("(k p) e -> p k e", p=P)).then_inc(const_in, 16)
            sp.dma_start(bg_b[:, :], bg.rearrange("(a d) -> a d", a=1).broadcast_to([SUB, E])).then_inc(const_in, 16)
            sp.dma_start(b1_sb[:, :, :], b1[:, :, :]).then_inc(const_in, 16)
            sp.dma_start(b2_sb[:, :], b2[:, :]).then_inc(const_in, 16)
            def load_chunk(j, c):
                g = 3 * c
                k0 = j * GPI + g
                if isinstance(j, int) and j == LASTJ and g + 2 >= LASTK:
                    n = LASTK - g
                    pairs = [(idx[:, g:g + n, :], src_g[:, k0:k0 + n, :]), (dst_i[:, g:g + n, :], dst_gr[:, k0:k0 + n, :]),
                             (idx_s[:, :], src_sh), (dst_s[:, :], dst_sh)]
                else:
                    pairs = [(idx[:, g:g + 3, :], src_g[:, bass.ds(k0, 3), :]), (dst_i[:, g:g + 3, :], dst_gr[:, bass.ds(k0, 3), :])]
                for to, at in pairs:
                    sp.dma_start(to, at).then_inc(idx_in[c], 16)

            for c in range(3):
                load_chunk(0, c)
            def load_raw(n):
                sp.dma_start(hid[:, n % 2, :].rearrange("p (k h) -> p k h", k=w_inner[n % 2]), w_raw[n % 2][n // 2])\
                    .then_inc(raw_in[n % 2], 16)
            load_raw(0)
            load_raw(1)
            for n in range(2, 2 * E):
                sp.wait_ge(squares_done, n - 1)
                load_raw(n)
            for c in range(XC):
                sp.wait_ge(xn_ready, c + 1)
                sp.dma_start(xn_rows[:, c * TC:(c + 1) * TC, :], xbuf[:, c * TC:(c + 1) * TC, :]).then_inc(xn_out[c], 16)
            sp.wait_ge(deg_done, 1)
            sp.dma_start(deg_tab.rearrange("(p c) -> p c", c=LO), deg_hl).then_inc(deg_out, 16)
            sp.wait_ge(deg_out, 16)
            sp.dma_start(deg[:, :], deg_tab[0:N].rearrange("(p c) -> p c", c=RT)).then_inc(deg_in, 16)
            sp.wait_ge(minmax_done, 2)
            sp.dma_start(min_tab.rearrange("(p s) -> p s", s=2), gmin).then_inc(minmax_out, 16)
            sp.dma_start(max_tab.rearrange("(p s) -> p s", s=2), gmax).then_inc(minmax_out, 16)
            sp.wait_ge(minmax_out, 32)
            sp.dma_start(base_i[:, :], min_tab.rearrange("(a g) -> a g", a=1)).then_inc(base_in, 16)
            sp.dma_start(max_i, max_tab.rearrange("(a g) -> a g", a=1)).then_inc(base_in, 16)
            sp.dma_start(base_bi, min_tab.rearrange("(a g) -> a g", a=1).broadcast_to([P, NG])).then_inc(base_in, 16)
            sp.wait_ge(r_ready, 2)
            sp.dma_start(r_tab.rearrange("(p c) -> p c", c=RT), r_small[:, :]).then_inc(r_out, 16)
            for c in range(YC):
                sp.wait_ge(y_scaled, c + 1)
                sp.dma_start(y_rows[:, c * TY:(c + 1) * TY, :], ybuf[c % YBUF]).then_inc(y_out[c % YBUF], 16)
            sp.wait_ge(r_out, 16)

            def load_expert(e):
                sp.dma_start(w1_sb[:, e], w_raw[0][e]).then_inc(w_in, 16)
                sp.dma_start(w2_sb[:, e], w_raw[1][e]).then_inc(w_in, 16)

            def load_block(b):
                at = b * NB
                sp.dma_start(x_blk[:, :, :], x[bass.ds(at, NB), :].rearrange("(s p) d -> p s d", s=2)).then_inc(blk_in, 16)
                sp.dma_start(xn_blk[:, :, :], xn_tab[bass.ds(at, NB), :].rearrange("(s p) d -> p s d", s=2)).then_inc(blk_in, 16)
                sp.dma_start(r_blk[:, :], r_tab[bass.ds(at, NB)].rearrange("(a n) -> a n", a=1).broadcast_to([P, NB])).then_inc(blk_in, 16)

            def store_block(b):
                sp.wait_ge(y_added, 8 * b + 8)
                sp.dma_start(out[bass.ds(b * NB, NB), :].rearrange("(s p) d -> p s d", s=2), outb[:, :, :]).then_inc(stored, 16)

            def iteration(j, edges, new, old):
                start = isinstance(j, int) and j == 0

                def load_parted(e):
                    if start:
                        if e:
                            sp.wait_ge(w_low, 2 * e)
                        load_raw(2 * e)
                        load_raw(2 * e + 1)
                if start:
                    sp.wait_ge(squares_done, 2 * E)
                for e in range(3):
                    load_parted(e)
                if edges:
                    sp.wait_ge(summed, GPI * j + 3)
                    load_chunk(j + 1, 0)
                if start:
                    for c in range(XC):
                        sp.wait_ge(xn_out[c], 16)
                if new:
                    sp.wait_ge(x1_done, j)
                if not (isinstance(j, int) and j >= NBLK):
                    load_block(j)
                for e in range(3, 6):
                    load_parted(e)
                if edges:
                    sp.wait_ge(summed, GPI * j + 6)
                    load_chunk(j + 1, 1)
                for e in range(6, E):
                    load_parted(e)
                if old:
                    store_block(j - 2)
                if edges:
                    sp.wait_ge(summed, GPI * j + 9)
                    load_chunk(j + 1, 2)

            fast = path_flag(sp)
            with sp.If(fast == 1):
                iteration(0, True, False, False)
                iteration(1, True, True, False)
                with sp.Fori(2, LASTJ - 1) as j:
                    iteration(j, True, True, True)
                iteration(LASTJ - 1, True, True, True)
                iteration(LASTJ, False, True, True)
                iteration(NBLK, False, True, True)
                store_block(NBLK - 1)
            with sp.Else():
                y_written(sp)
                for c in range(XC):
                    sp.wait_ge(xn_out[c], 16)
                for e in range(E):
                    load_expert(e)
                for c in range(3):
                    sp.wait_ge(idx_in[c], 32)
                with sp.Fori(0, FULL) as g:
                    sp.wait_ge(gen_acc, NBLK * g + ADD_INIT)
                    sp.dma_start(idx[:, 0:1, :], src_g[:, bass.ds(g, 1), :]).then_inc(gen_idx, 16)
                    sp.dma_start(dst_i[:, 0:1, :], dst_gr[:, bass.ds(g, 1), :]).then_inc(gen_idx, 16)
                sp.wait_ge(gen_acc, NBLK * FULL + ADD_INIT)
                sp.dma_start(idx_s[:, :], src_sh).then_inc(gen_idx, 16)
                sp.dma_start(dst_s[:, :], dst_sh).then_inc(gen_idx, 16)
                load_block(0)
                iteration(1, False, True, False)
                with sp.Fori(2, NBLK) as j:
                    iteration(j, False, True, True)
                iteration(NBLK, False, True, True)
                store_block(NBLK - 1)
            sp.wait_ge(stored, 16 * NBLK)

        @block.gpsimd
        def _(pool):
            nc.gpsimd.iota(iota_v, pattern=[[1, HI], [0, HC_COLS]], base=0, channel_multiplier=0,
                           allow_small_or_imprecise_dtypes=True).then_inc(pool_const, 1)
            nc.gpsimd.memset(zeros[:, :], 0.0).then_inc(pool_const, 1)
            nc.gpsimd.memset(eps_t[:, :], EPS).then_inc(pool_const, 1)
            nc.gpsimd.memset(ident[:, :], 0.0).then_inc(pool_const, 1)
            pool.wait_ge(pool_const, 4)
            nc.gpsimd.affine_select(out=ident[:, :], in_=ident[:, :], compare_op=ALU.not_equal, fill=1.0, base=0,
                                    pattern=[[-1, P]], channel_multiplier=1).then_inc(pool_const, 1)
            nc.gpsimd.memset(ones[:, :], 1.0).then_inc(pool_const, 1)
            for to, pat in ((iota_nb[:, :], [[1, NB]]),
                            (blk0[:, :], [[NB, NBLK]])):
                nc.gpsimd.iota(to, pattern=pat, base=0, channel_multiplier=0,
                               allow_small_or_imprecise_dtypes=True).then_inc(pool_const, 1)
            nc.gpsimd.iota(thr[:, 0:NBLK * GPI], pattern=[[NB, NBLK], [0, GPI]], base=0, channel_multiplier=0,
                           allow_small_or_imprecise_dtypes=True).then_inc(pool_const, 1)
            nc.gpsimd.memset(ones_f[:, :], 1.0).then_inc(pool_const, 1)
            pool.wait_ge(hist_done, 1)
            pool.wait_ge(minmax_done, 2)
            pool.wait_ge(squares_done, 2 * E + 1)
            pool.wait_ge(deg_out, 16)
            pool.wait_ge(minmax_out, 32)
            nc.gpsimd.memset(acc[:, :], 0.0).then_inc(acc_zero, 1)

            def gather_group(slot, k, sem_, last=False):
                tiles, rows = shape_of(k, last)
                for t in range(tiles):
                    ix = idx_s[:, t:t + 1] if tiles != TPG else idx[:, k, t:t + 1]
                    pool.indirect_dma_start(out=ring16[0:rows, slot, t, :], out_offset=None, in_=y_tab[:, :],
                                            in_offset=bass.IndirectOffsetOnAxis(ap=ix, axis=0)).then_inc(sem_, 16)

            def iteration(j, ks):
                for k in ks:
                    if k % 3 == 0:
                        pool.wait_ge(idx_in[k // 3], 32 * (j + 1) + (32 if isinstance(j, int) and j == LASTJ and k + 2 >= LASTK else 0))
                    if known(j * GPI + k - RING + 1, 1):
                        pool.wait_ge(summed, j * GPI + k - RING + 1)
                        settle(pool)
                    gather_group(k % RING, k, gathered[k % RING], isinstance(j, int) and j == LASTJ)

            y_written(pool)
            pool.wait_ge(r_out, 16)
            fast = path_flag(pool)
            with pool.If(fast == 1):
                iteration(0, range(GPI))
                with pool.Fori(1, LASTJ) as j:
                    iteration(j, range(GPI))
                iteration(LASTJ, range(LASTK + 1))
            with pool.Else():
                with pool.Fori(0, FULL) as g:
                    pool.wait_ge(gen_idx, 32 * g + 32)
                    settle(pool)
                    gather_group(0, 0, gen_rows)
                pool.wait_ge(gen_idx, 32 * NG)
                gather_group(0, LASTK, gen_rows, True)

        @block.scalar
        def _(act):
            for c in range(XC):
                act.wait_ge(x_in[c], 16)
                if c:
                    act.wait_ge(ln_sum, c)
                for t in range(c * TC, (c + 1) * TC):
                    ins = nc.scalar.activation(junk_t[:, t % TC, :], xbuf[:, t, :], ACT.Copy, accum_out=rowsum[:, t:t + 1])
                ins.then_inc(ln_sum, 1)
            act.wait_ge(ln_sum, XC)
            nc.scalar.activation(negmean[:, :], rowsum[:, :], ACT.Copy, scale=-1.0 / D).then_inc(ln_neg, 1)
            act.wait_ge(ln_neg, 1)
            for t in range(RT):
                ins = nc.scalar.activation(junk_t[:, t % TC, :], xbuf[:, t, :], ACT.Square, bias=negmean[:, t:t + 1],
                                           accum_out=rowsq[:, t:t + 1])
                if t % TC == TC - 1:
                    ins.then_inc(ln_sq, 1)
                    act.wait_ge(ln_sq, t // TC + 1)
            act.wait_ge(pool_const, 4)
            nc.scalar.activation(std[:, :], rowsq[:, :], ACT.Sqrt, scale=1.0 / D, bias=eps_t[:, 0:1]).then_inc(ln_std, 1)
            for n in range(2 * E):
                m = n % 2
                act.wait_ge(raw_in[m], 16 * (n // 2 + 1))
                if n >= 2:
                    act.wait_ge(squares_done, n - 1)
                nc.scalar.activation(junk_w[:, m, :], hid[:, m, :], ACT.Square, accum_out=squares[:, n:n + 1]).then_inc(squares_done, 1)
            act.wait_ge(const_in, 16 * 7)
            act.wait_ge(squares_done, 2 * E)
            nc.scalar.activation(junk_w[:, 0, 0:E * HCH].rearrange("p (e c) -> p e c", e=E), b1_sb[:, :, :], ACT.Square,
                                 accum_out=squares[:, 2 * E:2 * E + 1]).then_inc(squares_done, 1)
            act.wait_ge(ln_scale, 2)
            for t in range(RT):
                ins = nc.scalar.activation(xbuf[:, t, :], xbuf[:, t, :], ACT.Identity, scale=rstd[:, t:t + 1], bias=nmr[:, t:t + 1])
                if t % TC == TC - 1:
                    ins.then_inc(xn_ready, 1)

            def gelus(b, e, exact):
                n = 8 * b + e
                if known(n, 2):
                    act.wait_ge(y_ready, n - 1)
                for half in range(2):
                    act.wait_ge(hid_ready, 2 * n + half + 1)
                    if not exact and known(n, 1):
                        act.wait_ge(low_done, 2 * n + half - 1)
                    cs = slice(2 * half, 2 * half + 2)
                    for c in (2 * half, 2 * half + 1):
                        to = gelu[:, e % 2, c, :] if exact else gelu_f[:, c, :]
                        ins = nc.scalar.activation(to, ps_h[:, half, (c % 2) * NB:(c % 2 + 1) * NB], ACT.Gelu,
                                                   bias=b1_sb[:, e, c:c + 1], scale=1.0 if exact else 1.0 / (XSCALE * WSCALE))
                    if not exact:
                        ins.then_inc(gelu_raw, 1)
                        act.wait_ge(gelu_raw, 2 * n + half + 1)
                        ins = nc.scalar.activation(gelu16[:, e % 2, 0, cs, :], gelu_f[:, cs, :], ACT.Copy, scale=XSCALE)
                    ins.then_inc(gelu_done, 1)

            def iteration(j, new, old, exact=False):
                b = j - 1
                if old:
                    gelus(b - 1, SPLIT, exact)
                if new:
                    act.wait_ge(emb_ready, b + 1)
                    if known(b, 1):
                        act.wait_ge(ssq_ready, b)
                    for s in range(2):
                        ins = nc.scalar.activation(junk[:, s, :], emb[:, s, :], ACT.Square, accum_out=ssq[:, s:s + 1])
                    ins.then_inc(ssq_ready, 1)
                    act.wait_ge(ssq_floor, b + 1)
                    nc.scalar.activation(rn[:, :], ssq[:, :], ACT.Sqrt).then_inc(norm_ready, 1)
                    act.wait_ge(var_ready, b + 1)
                    nc.scalar.activation(rstd2[:, :], mv[:, :, 1], ACT.Sqrt, bias=eps_t[:, 0:1]).then_inc(std2_ready, 1)
                if old:
                    for e in range(SPLIT + 1, E):
                        gelus(b - 1, e, exact)
                if new:
                    act.wait_ge(xn2T_done, b + 1)
                    if not exact:
                        nc.scalar.activation(xn2_16[:, 0, :, :], xnT_ps, ACT.Copy, scale=XSCALE).then_inc(x16_high, 1)
                    nc.scalar.activation(xn2T[:, :, :], xnT_ps, ACT.Copy).then_inc(xn2T_ready, 1)
                    gelus(b, 0, exact)
                    act.wait_ge(maskT_done, b + 1)
                    nc.scalar.activation(maskT[:, :, :], maskT_ps, ACT.Copy).then_inc(maskT_ready, 1)
                    for e in range(1, SPLIT):
                        gelus(b, e, exact)

            act.wait_ge(deg_in, 16)
            nc.scalar.activation(deg[:, :], deg[:, :], ACT.Sqrt, scale=1.0 / YSCALE ** 2).then_inc(deg_root, 1)
            act.wait_ge(r_ready, 1)
            for t in range(RT):
                n = t // TY
                if t % TY == 0 and n >= YBUF:
                    act.wait_ge(y_out[n % YBUF], 16 * (n // YBUF))
                ins = nc.scalar.activation(ybuf[n % YBUF][:, t % TY, 0:D], xbuf[:, t, :], ACT.Copy, scale=r_col[:, t:t + 1])
                if t % TY == TY - 1:
                    ins.then_inc(y_high, 1)
            act.wait_ge(const_in, 16 * 7)
            fast = path_flag(act)
            with act.If(fast == 1):
                act.wait_ge(y_scaled, YC)
                y_written(act)
                for c in range(XC):
                    act.wait_ge(xn_out[c], 16)
                for n in range(2 * E):
                    act.wait_ge(raw_in[n % 2], 16 * (E + n // 2 + 1))
                    nc.scalar.activation(w_parts[n % 2][:, n // 2, 0, :], hid[:, n % 2, :], ACT.Copy, scale=WSCALE).then_inc(w_high, 1)
                iteration(1, True, False)
                with act.Fori(2, NBLK + 1) as j:
                    iteration(j, True, True)
                iteration(NBLK + 1, False, True)
            with act.Else():
                iteration(1, True, False, exact=True)
                with act.Fori(2, NBLK + 1) as j:
                    iteration(j, True, True, exact=True)
                iteration(NBLK + 1, False, True, exact=True)

        @block.tensor
        def _(pe):
            pe.wait_ge(pool_const, 2)
            nc.tensor.matmul(hist, zeros[0:SUB, 0:HI], zeros[0:SUB, 0:LO], start=True, stop=False)
            with pe.Fori(0, HCOL // (2 * HC_COLS)) as i:
                for b in range(2):
                    pe.wait_ge(hist_oh, 2 * i + b + 1)
                    for c in range(HC_COLS):
                        ins = nc.tensor.matmul(hist, oh_hi[:, b, :, c], oh_lo[:, b, :, c], start=False, stop=False)
                    ins.then_inc(hist_used, 1)
            nc.tensor.matmul(hist, zeros[0:SUB, 0:HI], zeros[0:SUB, 0:LO], start=False, stop=True).then_inc(hist_done, 1)
            pe.wait_ge(const_in, 16 * 7)
            pe.wait_ge(pool_const, 10)
            pe.wait_ge(deg_done, 1)
            pe.wait_ge(squares_done, 2 * E + 1)
            nc.tensor.matmul(ps_a[0:1, 0:2 * E + 1], ones_f[:, :], squares[:, :], start=True, stop=True).then_inc(square_sums, 1)
            pe.wait_ge(flag_ready, 1)

            def sum_group(j, k, last=False):
                g = GPI * j + k
                tiles, rows = shape_of(k, last)
                pe.wait_ge(onehot, g + 1)
                pe.wait_ge(gathered[k % RING], 16 * TPG * (3 * j + k // RING) + 16 * tiles)
                if known(g - RING + 1, 1):
                    pe.wait_ge(added, g - RING + 1)
                for h in range(KC):
                    for t in range(tiles):
                        for part in range(2):
                            at = part * D + h * P
                            nc.tensor.matmul(ps_g[:, k % RING, h * WIN:(h + 1) * WIN], ring16[0:rows, k % RING, t, at:at + P],
                                             oh[0:rows, k % RING, t, :], start=t + part == 0, stop=t + part == tiles)
                for t in range(tiles):
                    ins = nc.tensor.matmul(ps_g[:, k % RING, KC * WIN:(KC + 1) * WIN], ones[0:rows, :],
                                           oh[0:rows, k % RING, t, :], start=t == 0, stop=t == tiles - 1)
                ins.then_inc(summed, 1)

            def hidden(b, e, exact):
                n = 8 * b + e
                if e == 0:
                    pe.wait_ge(xn2T_ready, b + 1)
                for half in range(2):
                    if known(n, 1):
                        pe.wait_ge(gelu_done, 2 * n + half - 1)
                    for c in (2 * half, 2 * half + 1):
                        to = ps_h[:, half, (c % 2) * NB:(c % 2 + 1) * NB]
                        cs = slice(c * P, (c + 1) * P)
                        if exact:
                            pairs = [(w1_sb[:, e, k, cs], xn2T[:, k, :]) for k in range(KC)]
                        else:
                            pairs = [(w1_16[:, e, wp, k, cs], xn2_16[:, xp, k, :])
                                     for k in range(KC) for wp, xp in ((0, 0), (0, 1), (1, 0))]
                        for i, (w, m) in enumerate(pairs):
                            ins = nc.tensor.matmul(to, w, m, start=i == 0, stop=i == len(pairs) - 1)
                    ins.then_inc(hid_ready, 1)

            def output(b, e, exact):
                n = 8 * b + e
                pe.wait_ge(gelu_done if exact else low_done, 2 * n + 2)
                if known(n, 2):
                    pe.wait_ge(y_added, n - 1)
                for s in range(2):
                    ns = slice(s * SUB, (s + 1) * SUB)
                    if exact:
                        pairs = [(gelu[:, e % 2, c, ns], w2_sb[:, e, c, :]) for c in range(HCH)]
                    else:
                        pairs = [(gelu16[:, e % 2, gp, c, ns], w2_16[:, e, wp, c, :])
                                 for c in range(HCH) for gp, wp in ((0, 0), (0, 1), (1, 0))]
                    for i, (g, w) in enumerate(pairs):
                        ins = nc.tensor.matmul(ps_y[0:SUB, e % 2, s * D:(s + 1) * D], g, w, start=i == 0, stop=i == len(pairs) - 1)
                ins.then_inc(y_ready, 1)

            def transpose_block(rows, done):
                for s in range(2):
                    for k in range(KC):
                        ins = nc.tensor.transpose(xnT_ps[:, k, s * SUB:(s + 1) * SUB], rows[:, s, k * P:(k + 1) * P],
                                                  ident[0:SUB, 0:SUB])
                ins.then_inc(done, 1)

            def iteration(j, ks, new, old, last=False, exact=False):
                b = j - 1

                def grp(k):
                    if k in ks:
                        sum_group(j, k, last)
                if new:
                    pe.wait_ge(blk_in, 48 * (b + 1))
                    if known(b, 1):
                        pe.wait_ge(init_done, b)
                    transpose_block(xn_blk, xnT_ready)
                grp(0)
                if old:
                    hidden(b - 1, SPLIT, exact)
                if new:
                    pe.wait_ge(uv_ready, b + 1)
                    for s in range(2):
                        for m, t in enumerate((u_t, v_t)):
                            for k in range(KC):
                                ins = nc.tensor.matmul(z_ps[:, s, :], t[:, k, s * SUB:(s + 1) * SUB], gw_sb[:, m, k, :],
                                                       start=m + k == 0, stop=m + k == KC)
                    ins.then_inc(z_ready, 1)
                if old:
                    output(b - 1, SPLIT - 1, exact)
                grp(1)
                if old:
                    for e in range(SPLIT + 1, E - 1):
                        hidden(b - 1, e, exact)
                        output(b - 1, e - 1, exact)
                grp(2)
                if new:
                    pe.wait_ge(xn2_ready, b + 1)
                    transpose_block(emb, xn2T_done)
                if old:
                    hidden(b - 1, E - 1, exact)
                    output(b - 1, E - 2, exact)
                grp(3)
                if old:
                    output(b - 1, E - 1, exact)
                if new:
                    pe.wait_ge(xn2T_ready, b + 1)
                    for s in range(2):
                        for k in range(KC):
                            ins = nc.tensor.matmul(gate_ps[:, s, :], xn2T[:, k, s * SUB:(s + 1) * SUB], wg_sb[:, k, :],
                                                   start=k == 0, stop=k == KC - 1)
                    ins.then_inc(gate_done, 1)
                    if not exact:
                        pe.wait_ge(x16_ready, b + 1)
                    hidden(b, 0, exact)
                grp(4)
                if new:
                    pe.wait_ge(mask_ready, b + 1)
                    for s in range(2):
                        ins = nc.tensor.transpose(maskT_ps[:, s, :], mask[:, s, :], ident[0:SUB, 0:SUB])
                    ins.then_inc(maskT_done, 1)
                    hidden(b, 1, exact)
                    pe.wait_ge(maskT_ready, b + 1)
                    for s in range(2):
                        ins = nc.tensor.matmul(z_ps[:, s, :], maskT[:, s, :], b2_sb[:, :], start=True, stop=True)
                    ins.then_inc(b2_done, 1)
                    output(b, 0, exact)
                for k, e in ((5, 2), (6, 3), (7, 4)):
                    grp(k)
                    if new:
                        hidden(b, e, exact)
                        output(b, e - 1, exact)
                grp(8)

            fast = path_flag(pe)
            with pe.If(fast == 1):
                iteration(0, range(GPI), False, False)
                pe.wait_ge(w_low, 2 * E)
                iteration(1, range(GPI), True, False)
                with pe.Fori(2, LASTJ) as j:
                    iteration(j, range(GPI), True, True)
                iteration(LASTJ, range(LASTK + 1), True, True, last=True)
                iteration(NBLK, (), True, True)
                iteration(NBLK + 1, (), False, True)
            with pe.Else():
                def windows(g, tiles, rows):
                    with pe.Fori(0, NBLK) as w:
                        pe.wait_ge(gen_oh, NBLK * g + w + 1)
                        pe.wait_ge(gen_acc, NBLK * g + w + ADD_INIT)
                        for h in range(KC):
                            for t in range(tiles):
                                for part in range(2):
                                    at = part * D + h * P
                                    nc.tensor.matmul(ps_g[:, h, 0:NB], ring16[0:rows, 0, t, at:at + P], gen_hot[0:rows, t, :],
                                                     start=t + part == 0, stop=t + part == tiles)
                        for t in range(tiles):
                            ins = nc.tensor.matmul(ps_g[:, KC, 0:NB], ones[0:rows, :], gen_hot[0:rows, t, :],
                                                   start=t == 0, stop=t == tiles - 1)
                        ins.then_inc(gen_sum, 1)
                with pe.Fori(0, FULL) as g:
                    pe.wait_ge(gen_rows, 16 * TPG * g + 16 * TPG)
                    settle(pe)
                    windows(g, TPG, P)
                pe.wait_ge(gen_rows, 16 * TPG * FULL + 16 * SHORT_TILES)
                windows(FULL, SHORT_TILES, SHORT)
                pe.wait_ge(w_in, 32 * E)
                iteration(1, (), True, False, exact=True)
                with pe.Fori(2, NBLK + 1) as j:
                    iteration(j, (), True, True, exact=True)
                iteration(NBLK + 1, (), False, True, exact=True)

        @block.vector
        def _(dve):
            dve.wait_ge(src_in, 16)
            nc.vector.tensor_scalar(hi_i, src_i, 6, None, ALU.logical_shift_right).then_inc(hist_prep, 1)
            nc.vector.tensor_scalar(lo_i, src_i, LO - 1, None, ALU.bitwise_and).then_inc(hist_prep, 1)
            dve.wait_ge(hist_prep, 2)
            nc.vector.tensor_copy(hi_b, hi_i).then_inc(hist_prep, 1)
            nc.vector.tensor_copy(lo_b, lo_i).then_inc(hist_prep, 1)
            dve.wait_ge(hist_prep, 4)
            dve.wait_ge(pool_const, 1)

            def hot(col, b):
                for to, n, val in ((oh_hi, HI, hi_b), (oh_lo, LO, lo_b)):
                    v = val[:, bass.ds(col, HC_COLS)].rearrange("p (a c) -> p a c", a=1).broadcast_to([SUB, n, HC_COLS])
                    ins = nc.vector.tensor_tensor(to[:, b, :, :], iota_v[:, 0:n, :], v, ALU.is_equal)
                ins.then_inc(hist_oh, 1)

            HALF = HCOL // (2 * HC_COLS) // 2
            hot(0, 0)
            hot(HC_COLS, 1)
            with dve.Fori(1, HALF) as i:
                for b in range(2):
                    dve.wait_ge(hist_used, 2 * i + b - 1)
                    hot(i * 2 * HC_COLS + b * HC_COLS, b)
            dve.wait_ge(ln_std, 1)
            nc.vector.reciprocal(rstd[:, :], std[:, :]).then_inc(ln_scale, 1)
            dve.wait_ge(ln_scale, 1)
            nc.vector.tensor_tensor(nmr[:, :], negmean[:, :], rstd[:, :], ALU.mult).then_inc(ln_scale, 1)
            with dve.Fori(HALF, HCOL // (2 * HC_COLS)) as i:
                for b in range(2):
                    dve.wait_ge(hist_used, 2 * i + b - 1)
                    hot(i * 2 * HC_COLS + b * HC_COLS, b)
            dve.wait_ge(hist_done, 1)
            nc.vector.tensor_scalar(deg_hl, hist, 1.0, None, ALU.max).then_inc(deg_done, 1)
            dve.wait_ge(dst_in, 48)
            nc.vector.tensor_reduce(gmin, dst_g, AX.X, ALU.min).then_inc(minmax_done, 1)
            nc.vector.tensor_reduce(gmax, dst_g, AX.X, ALU.max).then_inc(minmax_done, 1)
            dve.wait_ge(deg_root, 1)
            nc.vector.reciprocal(r_col[:, :], deg[:, :]).then_inc(r_ready, 1)
            dve.wait_ge(r_ready, 1)
            nc.vector.tensor_scalar(r_small[:, :], r_col[:, :], YSCALE ** -2, None, ALU.mult).then_inc(r_ready, 1)
            for t in range(RT):
                n = t // TY
                if t % TY == 0:
                    dve.wait_ge(y_high, n + 1)
                ins = nc.vector.scalar_tensor_tensor(out=ybuf[n % YBUF][:, t % TY, D:2 * D], in0=xbuf[:, t, :],
                                                     scalar=r_col[:, t:t + 1], in1=ybuf[n % YBUF][:, t % TY, 0:D],
                                                     op0=ALU.mult, op1=ALU.subtract)
                if t % TY == TY - 1:
                    ins.then_inc(y_scaled, 1)
            dve.wait_ge(base_in, 48)
            dve.wait_ge(pool_const, 10)
            link = steps(dve, flag_chain, 0)
            link(nc.vector.tensor_copy(base_f[:, :], base_bi))
            link(nc.vector.tensor_tensor(span, max_i, base_f[0:1, :], ALU.subtract))
            link(nc.vector.memset(late, 0.0))
            link(nc.vector.tensor_tensor(late[:, LEAD:NG], thr[:, 0:NG - LEAD], base_f[0:1, LEAD:NG], ALU.subtract))
            link(nc.vector.tensor_reduce(flag_f[:, 0:1], span, AX.X, ALU.max))
            link(nc.vector.tensor_reduce(flag_f[:, 1:2], late, AX.X, ALU.max))
            dve.wait_ge(square_sums, 1)
            link(nc.vector.tensor_reduce(flag_f[:, 2:3], ps_a[0:1, 0:2 * E], AX.X, ALU.add))
            link(nc.vector.tensor_copy(flag_f[:, 3:4], ps_a[0:1, 2 * E:2 * E + 1]))
            for n, most in enumerate((float(WIN - 1), 0.0, P * W_SQUARES, B_SQUARES)):
                link(nc.vector.tensor_scalar(flag_f[:, n:n + 1], flag_f[:, n:n + 1], most, None, ALU.is_le))
            nc.vector.tensor_reduce(flag[:, :], flag_f[:, :], AX.X, ALU.min).then_inc(flag_ready, 1)
            dve.wait_ge(const_in, 16 * 7)
            dve.wait_ge(acc_zero, 1)

            def hot_group(j, k, last=False):
                g = GPI * j + k
                tiles, rows = shape_of(k, last)
                extra = 32 if isinstance(j, int) and j == LASTJ and 3 * (k // 3) + 2 >= LASTK else 0
                dve.wait_ge(idx_in[k // 3], 32 * (j + 1) + extra)
                if known(g - RING + 1, 1):
                    dve.wait_ge(summed, g - RING + 1)
                d = dst_s[:, :] if tiles != TPG else dst_i[:, k, :]
                base = base_f[0:rows, bass.ds(g, 1)].broadcast_to([rows, tiles])
                nc.vector.tensor_tensor(loc[0:rows, k % RING, 0:tiles], d, base, ALU.subtract).then_inc(loc_ready, 1)
                dve.wait_ge(loc_ready, g + 1)
                iw = iota_w[0:rows, :].rearrange("p (a w) -> p a w", a=1).broadcast_to([rows, tiles, WIN])
                lc = loc[0:rows, k % RING, 0:tiles].rearrange("p (t a) -> p t a", a=1).broadcast_to([rows, tiles, WIN])
                nc.vector.tensor_tensor(oh[0:rows, k % RING, 0:tiles, :], iw, lc, ALU.is_equal).then_inc(onehot, 1)

            def add_group(j, k):
                g = GPI * j + k
                first = dve.value_load(base_i[0:1, bass.ds(g, 1)], min_val=0, max_val=N - 1)
                dve.wait_ge(summed, g + 1)
                if known(g, 1):
                    dve.wait_ge(added, g)
                to = acc3[:, :, bass.ds(first, WIN)]
                fr = ps_g[:, k % RING, 0:3 * WIN].rearrange("p (c w) -> p c w", c=3)
                nc.vector.tensor_tensor(to, to, fr, ALU.add).then_inc(added, 1)

            def low_part(b, e):
                n = 8 * b + e
                for half in range(2):
                    dve.wait_ge(gelu_done, 2 * n + half + 1)
                    cs = slice(2 * half, 2 * half + 2)
                    nc.vector.scalar_tensor_tensor(out=gelu16[:, e % 2, 1, cs, :], in0=gelu_f[:, cs, :], scalar=XSCALE,
                                                   in1=gelu16[:, e % 2, 0, cs, :], op0=ALU.mult, op1=ALU.subtract)\
                        .then_inc(low_done, 1)

            def add_expert(b, e, exact):
                n = 8 * b + e
                dve.wait_ge(y_ready, n + 1)
                if e == 0:
                    dve.wait_ge(init_done, b + 1)
                else:
                    dve.wait_ge(y_added, n)
                to = outb if e == E - 1 else accy
                if e == E - 1 and known(b, 1):
                    dve.wait_ge(stored, 16 * b)
                for s in range(2):
                    ins = nc.vector.scalar_tensor_tensor(out=to[:, s, :], in0=ps_y[0:SUB, e % 2, s * D:(s + 1) * D],
                                                         scalar=(mask if exact else mask_s)[:, s, e:e + 1], in1=accy[:, s, :],
                                                         op0=ALU.mult, op1=ALU.add)
                ins.then_inc(y_added, 1)

            def iteration(j, ks, new, old, last=False, exact=False):
                b = j - 1

                def grp(k):
                    if k in ks:
                        add_group(j, k)
                        hot_next(k)
                        part_weights(k)

                def part_weights(k):
                    if isinstance(j, int) and j == 0 and k:
                        for n in (2 * k - 2, 2 * k - 1):
                            dve.wait_ge(w_high, n + 1)
                            nc.vector.scalar_tensor_tensor(out=w_parts[n % 2][:, n // 2, 1, :], in0=hid[:, n % 2, :], scalar=WSCALE,
                                                           in1=w_parts[n % 2][:, n // 2, 0, :], op0=ALU.mult, op1=ALU.subtract)\
                                .then_inc(w_low, 1)

                def hot_next(k):
                    if k in ks:
                        nk = k + 2
                        if nk < GPI:
                            if not last or nk <= LASTK:
                                hot_group(j, nk, last)
                        elif not last:
                            hot_group(j + 1, nk - GPI)
                def low(b_, e):
                    if not exact:
                        low_part(b_, e)
                if 0 in ks:
                    add_group(j, 0)
                if new:
                    link = steps(dve, uv_chain, 3 * b)
                    dve.wait_ge(blk_in, 48 * (b + 1))
                    dve.wait_ge(xnT_ready, b + 1)
                    if known(b, 1):
                        dve.wait_ge(z_ready, b)
                    if exact:
                        dve.wait_ge(gen_acc, NBLK * NG + ADD_INIT)
                    else:
                        dve.wait_ge(added, GPI * j + LEAD if ks else NG)
                    s_t = acc3[:, 0:KC, bass.ds(b * NB, NB)]
                    cnt = acc3[:, KC:KC + 1, bass.ds(b * NB, NB)].broadcast_to([P, KC, NB])
                    rb = r_blk[:, :].rearrange("p (a n) -> p a n", a=1).broadcast_to([P, KC, NB])
                    link(nc.vector.tensor_tensor(u_t[:, :, :], s_t, rb, ALU.mult))
                    link(nc.vector.tensor_tensor(v_t[:, :, :], u_t[:, :, :], xnT_ps, ALU.mult))
                    link(nc.vector.tensor_tensor(u_t[:, :, :], u_t[:, :, :], xnT_ps, ALU.add))
                    nc.vector.scalar_tensor_tensor(out=u_t[:, :, :], in0=cnt, scalar=0.0, in1=u_t[:, :, :],
                                                   op0=ALU.is_gt, op1=ALU.mult).then_inc(uv_ready, 1)
                hot_next(0)
                if old:
                    low(b - 1, SPLIT)
                if new:
                    link = steps(dve, z_chain, 6 * b)
                    dve.wait_ge(z_ready, b + 1)
                    bias = gb_b[:, :].rearrange("p (a d) -> p a d", a=1).broadcast_to([SUB, 2, D])
                    if known(b, 1):
                        dve.wait_ge(xn2T_done, b)
                    link(nc.vector.tensor_tensor(emb[:, :, :], z_ps, bias, ALU.add))
                    nc.vector.scalar_tensor_tensor(out=emb[:, :, :], in0=emb[:, :, :], scalar=0.01, in1=emb[:, :, :],
                                                   op0=ALU.mult, op1=ALU.max).then_inc(emb_ready, 1)
                if old:
                    add_expert(b - 1, SPLIT - 1, exact)
                if new:
                    dve.wait_ge(emb_ready, b + 1)
                    dve.wait_ge(ssq_ready, b + 1)
                    nc.vector.tensor_scalar(ssq[:, :], ssq[:, :], 1e-24, None, ALU.max).then_inc(ssq_floor, 1)
                    dve.wait_ge(norm_ready, b + 1)
                    link(nc.vector.reciprocal(rn[:, :], rn[:, :]))
                    for s in range(2):
                        ins = nc.vector.scalar_tensor_tensor(out=x1[:, s, :], in0=emb[:, s, :], scalar=rn[:, s:s + 1],
                                                             in1=x_blk[:, s, :], op0=ALU.mult, op1=ALU.add)
                        if s == 0:
                            link(ins)
                    ins.then_inc(x1_done, 1)
                    dve.wait_ge(x1_done, b + 1)
                    for s in range(2):
                        link(nc.vector.bn_stats(stats[:, s, :], x1[:, s, :]), settle)
                    for s in range(2):
                        ins = nc.vector.bn_aggr(mv[:, s, :], stats[:, s, :])
                    ins.then_inc(var_ready, 1)
                    dve.wait_ge(std2_ready, b + 1)
                    link(nc.vector.reciprocal(rstd2[:, :], rstd2[:, :]))
                    for s in range(2):
                        ins = nc.vector.tensor_scalar(emb[:, s, :], x1[:, s, :], mv[:, s, 0:1], rstd2[:, s:s + 1],
                                                      ALU.subtract, ALU.mult)
                    ins.then_inc(xn2_ready, 1)
                    assert link.at[0] == 6
                grp(1)
                if old:
                    for e in range(SPLIT + 1, E - 1):
                        low(b - 1, e)
                        add_expert(b - 1, e - 1, exact)
                grp(2)
                if old:
                    low(b - 1, E - 1)
                if new and not exact:
                    dve.wait_ge(x16_high, b + 1)
                    dve.wait_ge(xn2T_ready, b + 1)
                    nc.vector.scalar_tensor_tensor(out=xn2_16[:, 1, :, :], in0=xn2T[:, :, :], scalar=XSCALE, in1=xn2_16[:, 0, :, :],
                                                   op0=ALU.mult, op1=ALU.subtract).then_inc(x16_ready, 1)
                if old:
                    add_expert(b - 1, E - 2, exact)
                grp(3)
                if old:
                    add_expert(b - 1, E - 1, exact)
                if new:
                    link = steps(dve, gate_chain, 9 * b)
                    dve.wait_ge(gate_done, b + 1)
                    bias = bg_b[:, :].rearrange("p (a e) -> p a e", a=1).broadcast_to([SUB, 2, E])
                    link(nc.vector.tensor_tensor(score[:, :, :], gate_ps, bias, ALU.add), settle)
                    for s in range(2):
                        link(nc.vector.max(top[:, s, :], score[:, s, :]), settle)
                    for s in range(2):
                        link(nc.vector.max_index(topi[:, s, :], top[:, s, :], score[:, s, :]), settle)
                    link(nc.vector.tensor_copy(topf[:, :, :], topi[:, :, :]))
                    for s in range(2):
                        link(nc.vector.tensor_scalar(mask[:, s, :], iota_8[:, :], topf[:, s, 0:1], None, ALU.is_equal))
                        ins = nc.vector.scalar_tensor_tensor(out=mask[:, s, :], in0=iota_8[:, :], scalar=topf[:, s, 1:2],
                                                             in1=mask[:, s, :], op0=ALU.is_equal, op1=ALU.add)
                        if s == 0:
                            link(ins)
                    ins.then_inc(mask_ready, 1)
                    assert link.at[0] == 9
                    dve.wait_ge(mask_ready, b + 1)
                    if not exact:
                        nc.vector.tensor_scalar(mask_s[:, :, :], mask[:, :, :], 1.0 / (XSCALE * WSCALE), None, ALU.mult)\
                            .then_inc(mask_scaled, 1)
                        dve.wait_ge(mask_scaled, b + 1)
                    low(b, 0)
                grp(4)
                if new:
                    dve.wait_ge(b2_done, b + 1)
                    if known(b, 1):
                        dve.wait_ge(y_added, 8 * b)
                    nc.vector.tensor_tensor(accy[:, :, :], x1[:, :, :], z_ps, ALU.add).then_inc(init_done, 1)
                    low(b, 1)
                    add_expert(b, 0, exact)
                for k, e in ((5, 1), (6, 2), (7, 3)):
                    grp(k)
                    if new:
                        low(b, e + 1)
                        add_expert(b, e, exact)
                grp(8)

            fast = path_flag(dve)
            with dve.If(fast == 1):
                hot_group(0, 0)
                hot_group(0, 1)
                iteration(0, range(GPI), False, False)
                iteration(1, range(GPI), True, False)
                with dve.Fori(2, LASTJ) as j:
                    iteration(j, range(GPI), True, True)
                iteration(LASTJ, range(LASTK + 1), True, True, last=True)
                iteration(NBLK, (), True, True)
                iteration(NBLK + 1, (), False, True)
            with dve.Else():
                nc.vector.memset(loc[:, 1, :], 0.0).then_inc(gen_acc, ADD_INIT)

                def windows(g, d, tiles, rows):
                    with dve.Fori(0, NBLK) as w:
                        dve.wait_ge(gen_acc, NBLK * g + w + ADD_INIT)
                        first = blk0[0:rows, bass.ds(w, 1)].broadcast_to([rows, tiles])
                        nc.vector.tensor_tensor(loc[0:rows, 0, 0:tiles], d, first, ALU.subtract).then_inc(gen_loc, 1)
                        dve.wait_ge(gen_loc, NBLK * g + w + 1)
                        it = iota_nb[0:rows, :].rearrange("p (a w) -> p a w", a=1).broadcast_to([rows, tiles, NB])
                        lc = loc[0:rows, 0, 0:tiles].rearrange("p (t a) -> p t a", a=1).broadcast_to([rows, tiles, NB])
                        nc.vector.tensor_tensor(gen_hot[0:rows, 0:tiles, :], it, lc, ALU.is_equal).then_inc(gen_oh, 1)
                        dve.wait_ge(gen_sum, NBLK * g + w + 1)
                        to = acc3[:, :, bass.ds(w * NB, NB)]
                        nc.vector.tensor_tensor(to, to, ps_g[:, :, 0:NB], ALU.add).then_inc(gen_acc, 1)
                with dve.Fori(0, FULL) as g:
                    dve.wait_ge(gen_idx, 32 * g + 32)
                    settle(dve)
                    windows(g, dst_i[:, 0, :], TPG, P)
                dve.wait_ge(gen_idx, 32 * NG)
                windows(FULL, dst_s[:, :], SHORT_TILES, SHORT)
                iteration(1, (), True, False, exact=True)
                with dve.Fori(2, NBLK + 1) as j:
                    iteration(j, (), True, True, exact=True)
                iteration(NBLK + 1, (), False, True, exact=True)


_INS = ['x', 'src', 'dst', 'L0_gnn_W1', 'L0_gnn_W2', 'L0_gnn_b', 'L0_ffn_Wg', 'L0_ffn_bg', 'L0_ffn_W1', 'L0_ffn_b1',
        'L0_ffn_W2', 'L0_ffn_b2']


def kernel(**inputs):
    import numpy as _np
    import concourse.bacc as _bacc
    from concourse import mybir as _mybir
    from concourse.bass_utils import run_bass_kernel_spmd as _run

    nc = _bacc.Bacc("TRN2", target_bir_lowering=False, num_devices=1)
    arrays, args = {}, []
    for name in _INS:
        a = _np.ascontiguousarray(inputs[name])
        if name == 'src':
            a = a.view(_np.uint32)
        if name == 'L0_ffn_b1':
            a = _np.ascontiguousarray(a.reshape(a.shape[0], -1, 128).transpose(2, 0, 1))
        arrays[f"in_{name}"] = a
        args.append(nc.dram_tensor(f"in_{name}", a.shape, _mybir.dt.from_np(a.dtype), kind="ExternalInput").ap())
    shape = inputs['x'].shape
    args.append(nc.dram_tensor("out_0", shape, _mybir.dt.float32, kind="ExternalOutput").ap())
    bass_gnn_ffn(nc, *args)
    r = _run(nc, [arrays], core_ids=[0])
    return r.results[0]["out_0"]
```
